# Optimizing a Trainium2 kernel written in Bass

```python
import numpy as np
import jax
import jax.numpy as jnp

def _softmax(x, axis=-1):
    return jax.nn.softmax(x, axis=axis)

def _gelu(x):
    return jax.nn.gelu(x, approximate=True)

def _silu(x):
    return jax.nn.silu(x)

def _sigmoid(x):
    return jax.nn.sigmoid(x)

def _layernorm(x, axis=-1, eps=1e-05):
    m = jnp.mean(x, axis=axis, keepdims=True)
    v = jnp.var(x, axis=axis, keepdims=True)
    return (x - m) / jnp.sqrt(v + eps)

def _scatter_add(tgt, idx, src, axis=0):
    return tgt.at[idx].add(src)

def _segment_sum(src, seg, n):
    return jax.ops.segment_sum(src, seg, n)
kernel_name = 'mk_cond_resid_d2_seqx_r8_5cfb20'

def setup_inputs(seed: int=0):
    np.random.seed(seed)
    _w = jnp.asarray

    def _rec_inputs():
        import jax
        import jax.numpy as jnp
        _rk = jax.random.key(seed)
        x = -7.109e-05 + 0.9999 * jax.random.normal(jax.random.fold_in(_rk, 1), (32, 32, 256), jnp.float32)
        _lenS = 32 - jax.random.randint(jax.random.fold_in(_rk, 7), (32,), 0, max(1, 32 // 4) + 1, jnp.int32)
        _lenS2 = 32 - jax.random.randint(jax.random.fold_in(_rk, 8), (32,), 0, max(1, 32 // 4) + 1, jnp.int32)
        itok_B_0_7 = jax.random.randint(jax.random.fold_in(_rk, 11), (32,), 0, 8, jnp.int32)
        return (x, itok_B_0_7)
    x, itok_B_0_7 = _rec_inputs()

    def _L0_cond_setup():
        import jax, jax.numpy as jnp
        import numpy as np
        B, C, D, T, N_SUBJECTS = (128, 32, 32, 256, 8)
        key = jax.random.key(seed)
        kx, ks, kw = jax.random.split(key, 3)
        x = jax.random.normal(kx, (B, C, T), dtype=jnp.float32)
        subjects = jax.random.randint(ks, (B,), 0, N_SUBJECTS, dtype=jnp.int64)
        weights = jax.random.normal(kw, (N_SUBJECTS, C, D), dtype=jnp.float32) * (1.0 / C ** 0.5)
        return {'x': x, 'subjects': subjects, 'weights': weights}
    _L0_cond_all = _L0_cond_setup()
    _L0_cond_in = {k: v for k, v in _L0_cond_all.items() if k in ('weights',)}
    del _L0_cond_all

    def _L1_cond_setup():
        import jax, jax.numpy as jnp
        import numpy as np

        def _lora_linear(x, W, A, B, adapter_indices):
            base = jnp.einsum('bsd,df->bsf', x, W)
            Ai = A[adapter_indices]
            Bi = B[adapter_indices]
            lora = jnp.einsum('bsr,brf->bsf', jnp.einsum('bsd,bdr->bsr', x, Ai), Bi)
            return base + lora
        key = jax.random.key(seed)
        ks = jax.random.split(key, 10)
        H, I, N, R = (256, 1024, 8, 16)
        B, S = (4, 256)
        std_h = 1.0 / np.sqrt(H)
        std_i = 1.0 / np.sqrt(I)
        x = jax.random.normal(ks[0], (B, S, H), dtype=jnp.float32)
        adapter_indices = jax.random.randint(ks[1], (B,), 0, N, dtype=jnp.int32)
        Wg = jax.random.normal(ks[2], (H, I), dtype=jnp.float32) * std_h
        Wu = jax.random.normal(ks[3], (H, I), dtype=jnp.float32) * std_h
        Wd = jax.random.normal(ks[4], (I, H), dtype=jnp.float32) * std_i
        Ag = jax.random.normal(ks[5], (N, H, R), dtype=jnp.float32) * std_h
        Bg = jnp.zeros((N, R, I), dtype=jnp.float32) + 0.01
        Au = jax.random.normal(ks[6], (N, H, R), dtype=jnp.float32) * std_h
        Bu = jnp.zeros((N, R, I), dtype=jnp.float32) + 0.01
        Ad = jax.random.normal(ks[7], (N, I, R), dtype=jnp.float32) * std_i
        Bd = jnp.zeros((N, R, H), dtype=jnp.float32) + 0.01
        return {'x': x, 'Wg': Wg, 'Wu': Wu, 'Wd': Wd, 'Ag': Ag, 'Bg': Bg, 'Au': Au, 'Bu': Bu, 'Ad': Ad, 'Bd': Bd, 'adapter_indices': adapter_indices}
    _L1_cond_all = _L1_cond_setup()
    _L1_cond_in = {k: v for k, v in _L1_cond_all.items() if k in ('Wg', 'Wu', 'Wd', 'Ag', 'Bg', 'Au', 'Bu', 'Ad', 'Bd')}
    del _L1_cond_all
    return {'x': x, 'itok_B_0_7': itok_B_0_7, 'L0_cond_weights': _L0_cond_in['weights'], 'L1_cond_Wg': _L1_cond_in['Wg'], 'L1_cond_Wu': _L1_cond_in['Wu'], 'L1_cond_Wd': _L1_cond_in['Wd'], 'L1_cond_Ag': _L1_cond_in['Ag'], 'L1_cond_Bg': _L1_cond_in['Bg'], 'L1_cond_Au': _L1_cond_in['Au'], 'L1_cond_Bu': _L1_cond_in['Bu'], 'L1_cond_Ad': _L1_cond_in['Ad'], 'L1_cond_Bd': _L1_cond_in['Bd']}

def reference(x, itok_B_0_7, L0_cond_weights, L1_cond_Wg, L1_cond_Wu, L1_cond_Wd, L1_cond_Ag, L1_cond_Bg, L1_cond_Au, L1_cond_Bu, L1_cond_Ad, L1_cond_Bd):
    import jax
    import jax.numpy as jnp

    def _L0_cond_ref(x, subjects, weights):
        import jax, jax.numpy as jnp
        import numpy as np
        B, C, D, T, N_SUBJECTS = (128, 32, 32, 256, 8)
        w = weights[subjects]
        out = jnp.einsum('bct,bcd->bdt', x, w)
        return out

    def _L1_cond_ref(x, Wg, Wu, Wd, Ag, Bg, Au, Bu, Ad, Bd, adapter_indices):
        import jax, jax.numpy as jnp
        import numpy as np

        def _lora_linear(x, W, A, B, adapter_indices):
            base = jnp.einsum('bsd,df->bsf', x, W)
            Ai = A[adapter_indices]
            Bi = B[adapter_indices]
            lora = jnp.einsum('bsr,brf->bsf', jnp.einsum('bsd,bdr->bsr', x, Ai), Bi)
            return base + lora
        gate = _lora_linear(x, Wg, Ag, Bg, adapter_indices)
        up = _lora_linear(x, Wu, Au, Bu, adapter_indices)
        h = jax.nn.silu(gate) * up
        return _lora_linear(h, Wd, Ad, Bd, adapter_indices)
    x = x + _L0_cond_ref(x, itok_B_0_7, L0_cond_weights)
    x = x + _L1_cond_ref(x, L1_cond_Wg, L1_cond_Wu, L1_cond_Wd, L1_cond_Ag, L1_cond_Bg, L1_cond_Au, L1_cond_Bu, L1_cond_Ad, L1_cond_Bd, itok_B_0_7)
    return x

_drawn_inputs = setup_inputs


def setup_inputs(seed=0):
    import zlib

    import numpy as np

    out = dict(_drawn_inputs(seed))
    spreads = {'L1_cond_Bg': (0.009999999776482582, 0.2),
     'L1_cond_Bu': (0.009999999776482582, 0.2),
     'L1_cond_Bd': (0.009999999776482582, 0.2)}
    factors = {}
    for name, (base, spread) in spreads.items():
        noise = np.random.default_rng([zlib.crc32(name.encode()), seed]).standard_normal(out[name].shape)
        drawn = base * np.exp(spread * noise) if base else spread * noise
        out[name] = jnp.asarray(drawn.astype(out[name].dtype))
    for name, factor in factors.items():
        out[name] = (out[name] * factor).astype(out[name].dtype)
    return out
```

```python
from contextlib import ExitStack

import concourse.bass as bass
from concourse import mybir

F32 = mybir.dt.float32
F32R = mybir.dt.float32r
I32 = mybir.dt.int32
ALU = mybir.AluOpType
ACT = mybir.ActivationFunctionType
AX = mybir.AxisListType
ENG = mybir.EngineType


def cond_resid_kernel(nc, x, idx, w0, Wg, Wu, Wd, Ag, Bg, Au, Bu, Ad, Bd, out):
    S, C, D = x.shape
    N, _, R = Ag.shape
    I = Wg.shape[1]
    P = 128
    SG = P // C
    G = S // SG
    K = D // P
    CH = 512
    NC = I // CH
    T = CH // P
    KK = NC * T
    Q = G * NC
    LR = SG * R
    BW = 2 * I + D
    WX = 2 * LR + D
    assert N * R == P and 2 * LR == P and SG * C == P

    with ExitStack() as ctx:
        def sb(name, shape, dt=F32):
            return ctx.enter_context(nc.sbuf_tensor(name, shape, dt))

        def sem(name):
            return ctx.enter_context(nc.semaphore(name))

        def bank(name):
            return ctx.enter_context(nc.psum_tensor(name, [P, 512], F32))

        idx_i = sb("idx_i", [P, S], I32)
        idx_f = sb("idx_f", [P, G, SG])
        own = sb("own", [P, 2 * SG])
        idx_own = sb("idx_own", [P, G])
        n_row = sb("n_row", [P, N])
        onehot = sb("onehot", [P, G, N])
        idx_sel = sb("idx_sel", [P, G, SG])
        ident = sb("ident", [P, P])
        w0_rep = sb("w0_rep", [P, N, C])
        w0_own = sb("w0_own", [P, G, C])
        w0_diag = sb("w0_diag", [P, G, SG, C])
        x_sb = sb("x_sb", [P, G, D])
        x1 = sb("x1", [P, G, K, P])
        xT = sb("xT", [P, G, 4, P])
        xs_hi = sb("xs_hi", [P, 2, 4, P], F32R)
        xs_lo = sb("xs_lo", [P, 2, 4, P], F32R)
        a_raw = sb("a_raw", [P, 2, N, K, R])
        a_grp = sb("a_grp", [P, 2, K, 2, SG, R])
        xa = sb("xa", [P, 2, 2, SG, 2, R])
        w_raw = sb("w_raw", [P, NC, 2, K, CH])
        w_hi = sb("w_hi", [P, 2, K, I], F32R)
        w_lo = sb("w_lo", [P, 2, K, I], F32R)
        b_raw = sb("b_raw", [P, BW])
        b_hi = sb("b_hi", [P, BW], F32R)
        b_lo = sb("b_lo", [P, BW], F32R)
        b_grp = sb("b_grp", [P, 2, 2 * I], F32R)
        bd_grp = sb("bd_grp", [P, 2, D], F32R)
        ad_raw = sb("ad_raw", [P, N, KK, R])
        ad_hl = sb("ad_hl", [P, N, 2, KK, R], F32R)
        wdx = sb("wdx", [P, 2, KK, WX], F32R)
        sg = sb("sg", [P, 2, CH])
        h = sb("h", [P, 2, T, P])
        hT_hi = sb("hT_hi", [P, 2, T, P], F32R)
        hT_lo = sb("hT_lo", [P, 2, T, P], F32R)
        xd = sb("xd", [P, SG, 2, R])
        xd_hi = sb("xd_hi", [P, P], F32R)
        xd_lo = sb("xd_lo", [P, P], F32R)
        out_sb = sb("out_sb", [P, 2, D])
        w0_prod = sg[:, :, :].rearrange("p a b -> p (a b)")
        wd_raw = w_raw[:, 0].rearrange("p m k j -> p (m k j)").rearrange("p (c t d) -> p c t d", c=NC, t=T)

        b_dram = nc.dram_tensor("b_split", (N, 2, R, BW), F32, kind="Internal").ap()

        gate_ps = [bank(f"gate_ps{i}") for i in range(2)]
        up_ps = [bank(f"up_ps{i}") for i in range(2)]
        y_ps = [bank(f"y_ps{i}") for i in range(2)]
        hT_ps = bank("hT_ps")
        xdT_ps = bank("xdT_ps")
        l0_ps, x1T_ps, a_ps, xaT_ps = gate_ps, up_ps, y_ps, [hT_ps, xdT_ps]

        idx_in = sem("idx_in")
        w0_in = sem("w0_in")
        x_in = [sem(f"x_in{i}") for i in range(G // 2)]
        a_in = sem("a_in")
        b_in = sem("b_in")
        wg_in = [sem(f"wg_in{c}") for c in range(NC)]
        wu_in = [sem(f"wu_in{c}") for c in range(NC)]
        ad_in = sem("ad_in")
        wd_in = sem("wd_in")
        b_split_out = sem("b_split_out")
        b_grp_in = [sem(f"b_grp_in{i}") for i in range(2)]
        bd_grp_in = [sem(f"bd_grp_in{i}") for i in range(2)]
        out_sent = [sem(f"out_sent{i}") for i in range(2)]
        dve_step = sem("dve_step")
        ident_step = sem("ident_step")
        ident_ready = sem("ident_ready")
        n_row_ready = sem("n_row_ready")
        diag_zeroed = sem("diag_zeroed")
        w0_own_ready = sem("w0_own_ready")
        diag_ready = sem("diag_ready")
        l0_done = sem("l0_done")
        x1_ready = sem("x1_ready")
        x1T_done = sem("x1T_done")
        x1T_ready = sem("x1T_ready")
        a_grp_ready = sem("a_grp_ready")
        a_done = sem("a_done")
        xa_ready = sem("xa_ready")
        xaT_done = sem("xaT_done")
        xaT_ready = sem("xaT_ready")
        split_hi = sem("split_hi")
        split_lo = sem("split_lo")
        xs_hi_ready = sem("xs_hi_ready")
        xs_lo_ready = sem("xs_lo_ready")
        ad_grp_ready = sem("ad_grp_ready")
        gate_done = sem("gate_done")
        up_done = sem("up_done")
        silu_ready = sem("silu_ready")
        h_ready = sem("h_ready")
        hT_done = sem("hT_done")
        hT_hi_ready = sem("hT_hi_ready")
        hT_lo_ready = sem("hT_lo_ready")
        down_done = sem("down_done")
        xd_ready = sem("xd_ready")
        xdT_done = sem("xdT_done")
        xd_hi_ready = sem("xd_hi_ready")
        xd_lo_ready = sem("xd_lo_ready")
        y_done = sem("y_done")
        out_ready = sem("out_ready")

        def w_chunk(mat, c, arrived):
            cols = slice(c * CH, (c + 1) * CH)
            return (w_raw[:, c, mat], w_hi[:, mat, :, cols], w_lo[:, mat, :, cols], (arrived, 16))

        WD = slice(LR, LR + D)
        splits = [
            (b_raw[:], b_hi[:], b_lo[:], (b_in, 48)),
            w_chunk(0, 0, wg_in[0]),
            w_chunk(1, 0, wu_in[0]),
            w_chunk(0, 1, wg_in[1]),
            w_chunk(1, 1, wu_in[1]),
            (ad_raw[:], ad_hl[:, :, 0], ad_hl[:, :, 1], (ad_in, 16)),
            (wd_raw.rearrange("p c t d -> p (c t) d"), wdx[:, 0, :, WD], wdx[:, 1, :, WD], (wd_in, 16)),
        ]
        B_SPLIT, W_SPLIT, AD_SPLIT, WD_SPLIT = 1, {(0, 0): 2, (1, 0): 3, (0, 1): 4, (1, 1): 5}, 6, 7
        SPLIT_AT = {3: [0], 6: [1], 7: [2], 10: [3, 4, 5, 6]}
        STEPS = G + 3

        def by_tile(ap):
            return ap.rearrange("q (p k) -> q k p", k=K)

        def rank_cols(g):
            return slice(0, LR) if g % 2 == 0 else slice(D, D + LR)

        def out_cols(g):
            return slice(LR, LR + D) if g % 2 == 0 else slice(0, D)

        tok = x.rearrange("(g s) c d -> (s c) g d", g=G)
        out_tok = out.rearrange("(g s) c d -> g (s c) d", g=G)

        block = ctx.enter_context(nc.Block())

        @block.sync
        def _(sp):
            sp.dma_start(idx_i[:], idx.partition_broadcast(P)).then_inc(idx_in, 16)
            for s in range(SG):
                sp.dma_start(w0_rep[s * C:(s + 1) * C], w0.rearrange("n c d -> c n d")).then_inc(w0_in, 16)
            for i in range(G // 2):
                sp.dma_start(x_sb[:, 2 * i:2 * i + 2], tok[:, 2 * i:2 * i + 2]).then_inc(x_in[i], 16)
            for at, B in ((0, Bg), (I, Bu), (2 * I, Bd)):
                sp.dma_start(b_raw[:, at:at + B.shape[2]], B.rearrange("n r i -> (n r) i")).then_inc(b_in, 16)
            sp.wait_ge(split_hi, B_SPLIT)
            sp.dma_start(b_dram[:, 0].rearrange("n r i -> n r i"), b_hi[:].bitcast(F32)).then_inc(b_split_out, 16)
            sp.wait_ge(split_lo, B_SPLIT)
            sp.dma_start(b_dram[:, 1].rearrange("n r i -> n r i"), b_lo[:].bitcast(F32)).then_inc(b_split_out, 16)
            sp.wait_ge(b_split_out, 32)
            sp.wait_ge(idx_in, 16)

            def gather_b(g):
                b = g % 2
                _, ns = nc.values_load_multi_w_load_instructions(
                    idx_i[0:1, SG * g:SG * (g + 1)], engines=[ENG.SP], min_val=0, max_val=N - 1,
                    skip_runtime_bounds_check_because="adapter indices are 0..N-1")
                if g >= 2:
                    sp.wait_ge(up_done, NC * (g - 1))
                for s in range(SG):
                    rows = b_dram[bass.ds(ns[s], 1)].rearrange("a l r i -> (a l r) i")
                    sp.dma_start(b_grp[s * C:(s + 1) * C, b].bitcast(F32), rows[:, 0:2 * I]).then_inc(b_grp_in[b], 16)
                if g >= 2:
                    sp.wait_ge(y_done, g - 1)
                for s in range(SG):
                    rows = b_dram[bass.ds(ns[s], 1)].rearrange("a l r i -> (a l r) i")
                    sp.dma_start(bd_grp[s * C:(s + 1) * C, b].bitcast(F32), rows[:, 2 * I:BW]).then_inc(bd_grp_in[b], 16)

            def load_wd():
                sp.wait_ge(split_hi, W_SPLIT[1, 0])
                sp.wait_ge(split_lo, W_SPLIT[1, 0])
                sp.dma_start(wd_raw.rearrange("p c t d -> p c (t d)"),
                             Wd.rearrange("(c p t) d -> p c (t d)", c=NC, t=T)).then_inc(wd_in, 16)

            def store(g):
                sp.wait_ge(out_ready, g + 1)
                sp.dma_start(out_tok[g], out_sb[:, g % 2]).then_inc(out_sent[g % 2], 16)

            gather_b(0)
            load_wd()
            gather_b(1)
            for g in range(G):
                store(g)
                if g + 2 < G:
                    gather_b(g + 2)
            for b in range(2):
                sp.wait_ge(out_sent[b], 16 * (G // 2))

        @block.gpsimd
        def _(pool):
            pool.memset(ident[:], 0.0).then_inc(ident_step, 1)
            pool.wait_ge(ident_step, 1)
            pool.affine_select(out=ident[:], in_=ident[:], compare_op=ALU.not_equal, fill=1.0, base=0,
                               pattern=[[-1, P]], channel_multiplier=1).then_inc(ident_ready, 1)
            pool.memset(w0_diag[:], 0.0).then_inc(diag_zeroed, 1)

            pool.wait_ge(idx_in, 16)
            pool.wait_ge(a_in, 32)

            def adapters(g):
                _, ns = nc.values_load_multi_w_load_instructions(
                    idx_i[0:1, SG * g:SG * (g + 1)], engines=[ENG.Pool], min_val=0, max_val=N - 1,
                    skip_runtime_bounds_check_because="adapter indices are 0..N-1")
                return ns

            for g in range(G):
                ns = adapters(g)
                if g >= 2:
                    pool.wait_ge(a_done, g - 1)
                for s in range(SG):
                    last = pool.tensor_copy(
                        a_grp[:, g % 2, :, :, s, :],
                        a_raw[:, :, bass.ds(ns[s], 1), :, :].rearrange("p m a k r -> p k (m a) r"))
                last.then_inc(a_grp_ready, 1)
            pool.wait_ge(split_hi, AD_SPLIT)
            pool.wait_ge(split_lo, AD_SPLIT)
            for g in range(G):
                ns = adapters(g)
                at = 0 if g % 2 == 0 else LR + D
                if g >= 2:
                    pool.wait_ge(down_done, NC * (g - 1))
                for s in range(SG):
                    last = pool.tensor_copy(
                        wdx[:, :, :, at + s * R:at + (s + 1) * R].rearrange("p l t r -> p (l t) r"),
                        ad_hl[:, bass.ds(ns[s], 1)].rearrange("p a l t r -> p (a l t) r"))
                last.then_inc(ad_grp_ready, 1)

        @block.scalar
        def _(act):
            for m, A in enumerate((Ag, Au)):
                act.dma_start(a_raw[:, m].rearrange("p n k r -> p n (k r)"),
                              A.rearrange("n (p k) r -> p n (k r)", k=K)).then_inc(a_in, 16)
            for c in range(NC):
                for m, (W, arrived) in enumerate(((Wg, wg_in), (Wu, wu_in))):
                    act.dma_start(w_raw[:, c, m], W.rearrange("(p k) i -> p k i", k=K)[:, :, c * CH:(c + 1) * CH]
                                  ).then_inc(arrived[c], 16)
            act.dma_start(ad_raw[:].rearrange("p n (c t) r -> p n c (t r)", c=NC),
                          Ad.rearrange("n (c p t) r -> p n c (t r)", c=NC, t=T)).then_inc(ad_in, 16)

            act.wait_ge(diag_zeroed, 1)
            for half in range(2):
                act.wait_ge(w0_own_ready, half + 1)
                gs = slice(half * G // 2, (half + 1) * G // 2)
                for s in range(SG):
                    rows = slice(s * C, (s + 1) * C)
                    last = act.activation(w0_diag[rows, gs, s, :], w0_own[rows, gs, :], ACT.Copy)
                last.then_inc(diag_ready, 1)

            def x1T_out(g):
                act.wait_ge(x1T_done, g + 1)
                act.activation(xT[:, g, 0:K], x1T_ps[g % 2][:, 0:K * P].rearrange("p (k t) -> p k t", k=K),
                               ACT.Copy).then_inc(x1T_ready, 1)

            def xaT_out(g):
                act.wait_ge(xaT_done, g + 1)
                act.activation(xT[:, g, K:K + 2], xaT_ps[g % 2][:, 0:2 * P].rearrange("p (m t) -> p m t", m=2),
                               ACT.Copy).then_inc(xaT_ready, 1)

            def weight_hi(i):
                raw, hi, _, (arrived, count) = splits[i]
                act.wait_ge(arrived, count)
                act.activation(hi, raw, ACT.Copy).then_inc(split_hi, 1)

            for t in range(STEPS):
                if 1 <= t <= G:
                    x1T_out(t - 1)
                if 3 <= t:
                    xaT_out(t - 3)
                if t == STEPS - 1:
                    group_hi_at_start = True
                    act.wait_ge(x1T_ready, 1)
                    act.wait_ge(xaT_ready, 1)
                    act.activation(xs_hi[:, 0], xT[:, 0], ACT.Copy).then_inc(xs_hi_ready, 1)
                for i in SPLIT_AT.get(t, []):
                    weight_hi(i)

            def group_hi(g):
                act.wait_ge(x1T_ready, g + 1)
                act.wait_ge(xaT_ready, g + 1)
                if g >= 2:
                    act.wait_ge(up_done, NC * (g - 1))
                act.activation(xs_hi[:, g % 2], xT[:, g], ACT.Copy).then_inc(xs_hi_ready, 1)

            def silu(q):
                act.wait_ge(gate_done, q + 1)
                if q >= 2:
                    act.wait_ge(h_ready, q - 1)
                act.activation(sg[:, q % 2], gate_ps[q % 2][:], ACT.Silu).then_inc(silu_ready, 1)

            def hidden_hi(q):
                act.wait_ge(hT_done, q + 1)
                if q >= 2:
                    act.wait_ge(down_done, q - 1)
                act.activation(hT_hi[:, q % 2], hT_ps[:].rearrange("p (t n) -> p t n", t=T),
                               ACT.Copy).then_inc(hT_hi_ready, 1)

            def rank_hi(g):
                act.wait_ge(xdT_done, g + 1)
                if g >= 1:
                    act.wait_ge(y_done, g)
                act.activation(xd_hi[:], xdT_ps[:, 0:P], ACT.Copy).then_inc(xd_hi_ready, 1)

            for q in range(Q + 1):
                g, c = q // NC, q % NC
                if q < Q:
                    silu(q)
                if q >= 1:
                    hidden_hi(q - 1)
                if c == 0 and g + 1 < G:
                    group_hi(g + 1)
                if c == 1 and g >= 1:
                    rank_hi(g - 1)
            rank_hi(G - 1)

        @block.tensor
        def _(pe):
            def l0(g):
                if g % (G // 2) == 0:
                    pe.wait_ge(diag_ready, g // (G // 2) + 1)
                if g % 2 == 0:
                    pe.wait_ge(x_in[g // 2], 16)
                if g >= 2:
                    pe.wait_ge(x1_ready, g - 1)
                pe.matmul(l0_ps[g % 2][:, 0:D], w0_diag[:, g].rearrange("p s c -> p (s c)"), x_sb[:, g],
                          start=True, stop=True).then_inc(l0_done, 1)

            def x1_turn(g):
                if g == 0:
                    pe.wait_ge(ident_ready, 1)
                pe.wait_ge(x1_ready, g + 1)
                if g >= 2:
                    pe.wait_ge(x1T_ready, g - 1)
                for k in range(K):
                    mm = pe.transpose(x1T_ps[g % 2][:, k * P:(k + 1) * P], x1[:, g, k], ident[:])
                mm.then_inc(x1T_done, 1)

            def rank_in(g):
                pe.wait_ge(x1T_ready, g + 1)
                pe.wait_ge(a_grp_ready, g + 1)
                if g >= 2:
                    pe.wait_ge(xa_ready, g - 1)
                for k in range(K):
                    mm = pe.matmul(a_ps[g % 2][:, 0:2 * LR], xT[:, g, k],
                                   a_grp[:, g % 2, k].rearrange("p m s r -> p (m s r)"),
                                   start=(k == 0), stop=(k == K - 1))
                mm.then_inc(a_done, 1)

            def xa_turn(g):
                pe.wait_ge(xa_ready, g + 1)
                if g >= 2:
                    pe.wait_ge(xaT_ready, g - 1)
                for m in range(2):
                    mm = pe.transpose(xaT_ps[g % 2][:, m * P:(m + 1) * P],
                                      xa[:, g % 2, m].rearrange("p s l r -> p (s l r)"), ident[:])
                mm.then_inc(xaT_done, 1)

            for t in range(STEPS):
                if t < G:
                    l0(t)
                if 1 <= t <= G:
                    x1_turn(t - 1)
                if 2 <= t <= G + 1:
                    rank_in(t - 2)
                if 3 <= t:
                    xa_turn(t - 3)

            def half_mlp(q, mat, ps, done):
                g, c = q // NC, q % NC
                cols = slice(c * CH, (c + 1) * CH)
                b = g % 2
                if g == 0:
                    pe.wait_ge(split_hi, W_SPLIT[mat, c])
                    pe.wait_ge(split_lo, W_SPLIT[mat, c])
                for k in range(K):
                    pe.matmul(ps, xs_hi[:, b, k], w_hi[:, mat, k, cols], start=(k == 0), stop=False)
                    pe.matmul(ps, xs_hi[:, b, k], w_lo[:, mat, k, cols], start=False, stop=False)
                    pe.matmul(ps, xs_lo[:, b, k], w_hi[:, mat, k, cols], start=False, stop=False)
                if c == 0 and mat == 0:
                    pe.wait_ge(b_grp_in[b], 16 * SG * (g // 2 + 1))
                rows = b_grp[:, b, mat * I + c * CH:mat * I + (c + 1) * CH]
                pe.matmul(ps, xs_hi[:, b, K + mat], rows, start=False, stop=False)
                pe.matmul(ps, xs_lo[:, b, K + mat], rows, start=False, stop=True).then_inc(done, 1)

            def gate(q):
                g, c = q // NC, q % NC
                if c == 0:
                    pe.wait_ge(xs_hi_ready, g + 1)
                    pe.wait_ge(xs_lo_ready, g + 1)
                if q >= 2:
                    pe.wait_ge(silu_ready, q - 1)
                half_mlp(q, 0, gate_ps[q % 2][:], gate_done)

            def up(q):
                if q >= 2:
                    pe.wait_ge(h_ready, q - 1)
                half_mlp(q, 1, up_ps[q % 2][:], up_done)

            def hidden_turn(q):
                pe.wait_ge(h_ready, q + 1)
                if q == 0:
                    pe.wait_ge(xaT_ready, G)
                else:
                    pe.wait_ge(hT_hi_ready, q)
                    pe.wait_ge(hT_lo_ready, q)
                for t in range(T):
                    mm = pe.transpose(hT_ps[:, t * P:(t + 1) * P], h[:, q % 2, t], ident[:])
                mm.then_inc(hT_done, 1)

            def down(q):
                g, c = q // NC, q % NC
                if c == 0:
                    pe.wait_ge(ad_grp_ready, g + 1)
                    if g == 0:
                        pe.wait_ge(split_hi, WD_SPLIT)
                        pe.wait_ge(split_lo, WD_SPLIT)
                    if g >= 2:
                        pe.wait_ge(out_ready, g - 1)
                pe.wait_ge(hT_hi_ready, q + 1)
                pe.wait_ge(hT_lo_ready, q + 1)
                at = 0 if g % 2 == 0 else LR
                ps = y_ps[g % 2][:, 0:LR + D]
                for t in range(T):
                    kk = c * T + t
                    hi, lo = (wdx[:, l, kk, at:at + LR + D] for l in range(2))
                    pe.matmul(ps, hT_hi[:, q % 2, t], hi, start=(kk == 0), stop=False)
                    pe.matmul(ps, hT_hi[:, q % 2, t], lo, start=False, stop=False)
                    mm = pe.matmul(ps, hT_lo[:, q % 2, t], hi, start=False, stop=(kk == KK - 1))
                mm.then_inc(down_done, 1)

            def rank_turn(g):
                pe.wait_ge(xd_ready, g + 1)
                if g >= 1:
                    pe.wait_ge(xd_hi_ready, g)
                    pe.wait_ge(xd_lo_ready, g)
                pe.transpose(xdT_ps[:, 0:P], xd[:].rearrange("p s l r -> p (s l r)"), ident[:]).then_inc(xdT_done, 1)

            def rank_out(g):
                pe.wait_ge(bd_grp_in[g % 2], 16 * SG * (g // 2 + 1))
                pe.wait_ge(xd_hi_ready, g + 1)
                pe.wait_ge(xd_lo_ready, g + 1)
                ps = y_ps[g % 2][:, out_cols(g)]
                pe.matmul(ps, xd_hi[:], bd_grp[:, g % 2], start=False, stop=False, skip_group_check=True)
                pe.matmul(ps, xd_lo[:], bd_grp[:, g % 2], start=False, stop=True,
                          skip_group_check=True).then_inc(y_done, 1)

            for q in range(Q + 1):
                g, c = q // NC, q % NC
                if q < Q:
                    gate(q)
                if q >= 1:
                    hidden_turn(q - 1)
                if c == 1 and g >= 1:
                    rank_turn(g - 1)
                if q < Q:
                    up(q)
                if c == 1 and g >= 1:
                    rank_out(g - 1)
                if q >= 1:
                    down(q - 1)
            rank_turn(G - 1)
            rank_out(G - 1)

        @block.vector
        def _(dve):
            steps = 0

            def chain(ins):
                nonlocal steps
                steps += 1
                ins.then_inc(dve_step, 1)
                dve.wait_ge(dve_step, steps)

            for n in range(N):
                dve.memset(n_row[:, n:n + 1], float(n))
            chain(dve.memset(own[:], 0.0))
            for s in range(SG):
                last = dve.memset(own[s * C:(s + 1) * C, s:2 * SG:SG], 1.0)
            chain(last)
            dve.wait_ge(idx_in, 16)
            chain(dve.tensor_copy(idx_f[:].rearrange("p g s -> p (g s)"), idx_i[:]))
            own_g = own[:, 0:SG].unsqueeze(1).to_broadcast([P, G, SG])
            chain(dve.tensor_tensor(idx_sel[:], idx_f[:], own_g, ALU.mult))
            chain(dve.tensor_reduce(idx_own[:], idx_sel[:], AX.X, ALU.add))
            chain(dve.tensor_tensor(onehot[:], idx_own[:].unsqueeze(2).to_broadcast([P, G, N]),
                                    n_row[:].unsqueeze(1).to_broadcast([P, G, N]), ALU.is_equal))
            dve.wait_ge(w0_in, 16 * SG)
            GH = G // 2
            for half in range(2):
                gs = slice(half * GH, (half + 1) * GH)
                prod = w0_prod[:, 0:GH * C * N].rearrange("p (g c n) -> p g c n", g=GH, c=C)
                for g in range(GH):
                    last = dve.tensor_tensor(
                        prod[:, g], w0_rep[:].rearrange("p n c -> p c n"),
                        onehot[:, half * GH + g].unsqueeze(1).to_broadcast([P, C, N]), ALU.mult)
                chain(last)
                ins = dve.tensor_reduce(w0_own[:, gs], prod, AX.X, ALU.add)
                ins.then_inc(w0_own_ready, 1)
                if half == 0:
                    dve.wait_ge(w0_own_ready, 1)

            def x1_add(g):
                dve.wait_ge(l0_done, g + 1)
                dve.tensor_tensor(x1[:, g], by_tile(l0_ps[g % 2][:, 0:D]), by_tile(x_sb[:, g]),
                                  ALU.add).then_inc(x1_ready, 1)

            def xa_place(g):
                dve.wait_ge(a_done, g + 1)
                if g >= 2:
                    dve.wait_ge(xaT_done, g - 1)
                dve.tensor_tensor(
                    xa[:, g % 2].rearrange("p m s l r -> p (m s) l r"),
                    a_ps[g % 2][:, 0:2 * LR].rearrange("p (j r) -> p j r", r=R).unsqueeze(2)
                    .to_broadcast([P, 2 * SG, 2, R]),
                    own[:].unsqueeze(2).unsqueeze(3).to_broadcast([P, 2 * SG, 2, R]), ALU.mult).then_inc(xa_ready, 1)

            def weight_lo(i):
                raw, hi, lo, _ = splits[i]
                dve.wait_ge(split_hi, i + 1)
                dve.tensor_tensor(lo, raw, hi.bitcast(F32), ALU.subtract).then_inc(split_lo, 1)

            def group_lo(g):
                dve.wait_ge(xs_hi_ready, g + 1)
                dve.tensor_tensor(xs_lo[:, g % 2], xT[:, g], xs_hi[:, g % 2].bitcast(F32),
                                  ALU.subtract).then_inc(xs_lo_ready, 1)

            for t in range(STEPS):
                if t < G:
                    x1_add(t)
                if 2 <= t <= G + 1:
                    xa_place(t - 2)
                if t == STEPS - 1:
                    group_lo(0)
                for i in SPLIT_AT.get(t, []):
                    weight_lo(i)

            def hidden_lo(q):
                dve.wait_ge(hT_hi_ready, q + 1)
                dve.tensor_tensor(hT_lo[:, q % 2], hT_ps[:].rearrange("p (t n) -> p t n", t=T),
                                  hT_hi[:, q % 2].bitcast(F32), ALU.subtract).then_inc(hT_lo_ready, 1)

            def hidden(q):
                dve.wait_ge(silu_ready, q + 1)
                dve.wait_ge(up_done, q + 1)
                if q >= 2:
                    dve.wait_ge(hT_done, q - 1)
                dve.tensor_tensor(h[:, q % 2], up_ps[q % 2][:].rearrange("n (p t) -> n t p", t=T),
                                  sg[:, q % 2].rearrange("n (p t) -> n t p", t=T), ALU.mult).then_inc(h_ready, 1)

            def rank_place(g):
                dve.wait_ge(down_done, NC * (g + 1))
                if g >= 1:
                    dve.wait_ge(xdT_done, g)
                dve.tensor_tensor(
                    xd[:], y_ps[g % 2][:, rank_cols(g)].rearrange("p (s r) -> p s r", s=SG).unsqueeze(2)
                    .to_broadcast([P, SG, 2, R]),
                    own[:, 0:SG].unsqueeze(2).unsqueeze(3).to_broadcast([P, SG, 2, R]), ALU.mult).then_inc(xd_ready, 1)

            def rank_lo(g):
                dve.wait_ge(xd_hi_ready, g + 1)
                dve.tensor_tensor(xd_lo[:], xdT_ps[:, 0:P], xd_hi[:].bitcast(F32), ALU.subtract).then_inc(xd_lo_ready, 1)

            def final(g):
                dve.wait_ge(y_done, g + 1)
                if g >= 2:
                    dve.wait_ge(out_sent[g % 2], 16 * (g // 2))
                dve.tensor_tensor(by_tile(out_sb[:, g % 2]), by_tile(y_ps[g % 2][:, out_cols(g)]), x1[:, g],
                                  ALU.add).then_inc(out_ready, 1)

            for q in range(Q + 1):
                g, c = q // NC, q % NC
                if c == 1 and g >= 1:
                    rank_place(g - 1)
                if q >= 1:
                    hidden_lo(q - 1)
                if c == 1 and g >= 1:
                    rank_lo(g - 1)
                if q < Q:
                    hidden(q)
                if c == 1 and g >= 1:
                    final(g - 1)
                if c == 0 and g + 1 < G:
                    group_lo(g + 1)
            rank_place(G - 1)
            rank_lo(G - 1)
            final(G - 1)


_INS = ["x", "itok_B_0_7", "L0_cond_weights", "L1_cond_Wg", "L1_cond_Wu", "L1_cond_Wd", "L1_cond_Ag", "L1_cond_Bg",
        "L1_cond_Au", "L1_cond_Bu", "L1_cond_Ad", "L1_cond_Bd"]


def kernel(**inputs):
    import numpy as _np
    import concourse.bacc as _bacc
    from concourse import mybir as _mybir
    from concourse.bass_utils import run_bass_kernel_spmd as _run

    nc = _bacc.Bacc("TRN2", target_bir_lowering=False, num_devices=1)
    arrays, args = {}, []
    for name in _INS:
        a = _np.ascontiguousarray(inputs[name])
        arrays[f"in_{name}"] = a
        args.append(nc.dram_tensor(f"in_{name}", a.shape, _mybir.dt.from_np(a.dtype), kind="ExternalInput").ap())
    shape = inputs["x"].shape
    args.append(nc.dram_tensor("out_dram", shape, _mybir.dt.float32, kind="ExternalOutput").ap())
    cond_resid_kernel(nc, *args)
    r = _run(nc, [arrays], core_ids=[0])
    return r.results[0]["out_dram"]
```

```python
from contextlib import ExitStack

import concourse.bass as bass
from concourse import mybir

F32 = mybir.dt.float32
F32R = mybir.dt.float32r
I32 = mybir.dt.int32
ALU = mybir.AluOpType
ACT = mybir.ActivationFunctionType
AX = mybir.AxisListType
ENG = mybir.EngineType


def cond_resid_kernel(nc, x, idx, w0, Wg, Wu, Wd, A_in, B_all, A_down, out):
    S, C, D = x.shape
    N, R2, BW = B_all.shape
    R = R2 // 2
    I = Wg.shape[1]
    P = 128
    SG = P // C
    G = S // SG
    K = D // P
    CH = 512
    NC = I // CH
    T = CH // P
    KK = NC * T
    Q = G * NC
    LR = SG * R
    WX = 2 * LR + D
    assert 2 * LR == P and SG * C == P and 2 * R == C and BW == 2 * I + D

    with ExitStack() as ctx:
        def sb(name, shape, dt=F32):
            return ctx.enter_context(nc.sbuf_tensor(name, shape, dt))

        def sem(name):
            return ctx.enter_context(nc.semaphore(name))

        def bank(name):
            return ctx.enter_context(nc.psum_tensor(name, [P, 512], F32))

        idx_i = sb("idx_i", [P, S], I32)
        idx_f = sb("idx_f", [P, G, SG])
        own = sb("own", [P, 2 * SG])
        idx_own = sb("idx_own", [P, G])
        n_row = sb("n_row", [P, N])
        act_warm = sb("act_warm", [P, 1])
        onehot = sb("onehot", [P, G, N])
        idx_sel = sb("idx_sel", [P, G, SG])
        ident = sb("ident", [P, P])
        w0_rep = sb("w0_rep", [P, C, N])
        w0_own = sb("w0_own", [P, G, C])
        w0_diag = sb("w0_diag", [P, G, SG, C])
        x_sb = sb("x_sb", [P, G, D])
        x1 = sb("x1", [P, G, K, P])
        xT = sb("xT", [P, G, 4, P])
        xs_hi = sb("xs_hi", [P, 2, 4, P], F32R)
        xs_lo = sb("xs_lo", [P, 2, 4, P], F32R)
        a_raw = sb("a_raw", [P, 2, N, K, R])
        a_grp = sb("a_grp", [P, 2, K, 2, SG, R])
        xa = sb("xa", [P, 2, 2, SG, 2, R])
        w_raw = sb("w_raw", [P, NC, 2, K, CH])
        w_hi = sb("w_hi", [P, 2, K, I], F32R)
        w_lo = sb("w_lo", [P, 2, K, I], F32R)
        row = sb("row", [P, 1], I32)
        row_bit = sb("row_bit", [P, 1], I32)
        is_lo = sb("is_lo", [P, 1])
        sign_lo = sb("sign_lo", [P, 1])
        b_raw = sb("b_raw", [P, 2, 2 * I])
        bd_raw = sb("bd_raw", [P, 2, D])
        b_grp = sb("b_grp", [P, 2, 2 * I], F32R)
        bd_grp = sb("bd_grp", [P, 2, D], F32R)
        ad_raw = sb("ad_raw", [P, N, KK, R])
        ad_hl = sb("ad_hl", [P, N, 2, KK, R], F32R)
        wd_raw = sb("wd_raw", [P, NC, T, D])
        wdx = sb("wdx", [P, 2, KK, WX], F32R)
        sg = sb("sg", [P, 2, CH])
        h = sb("h", [P, 2, T, P])
        hT_hi = sb("hT_hi", [P, 2, T, P], F32R)
        hT_lo = sb("hT_lo", [P, 2, T, P], F32R)
        xd = sb("xd", [P, SG, 2, R])
        xd_hi = sb("xd_hi", [P, P], F32R)
        xd_lo = sb("xd_lo", [P, P], F32R)
        out_sb = sb("out_sb", [P, 2, D])
        w0_prod = sg
        gate_ps = [bank(f"gate_ps{i}") for i in range(2)]
        up_ps = [bank(f"up_ps{i}") for i in range(2)]
        y_ps = [bank(f"y_ps{i}") for i in range(2)]
        hT_ps = bank("hT_ps")
        xdT_ps = bank("xdT_ps")
        l0_ps, x1T_ps, a_ps, xaT_ps = gate_ps, up_ps, y_ps, [hT_ps, xdT_ps]

        idx_in = sem("idx_in")
        w0_in = sem("w0_in")
        x_in = [sem(f"x_in{i}") for i in range(G // 2)]
        a_in = sem("a_in")
        wg_in = [sem(f"wg_in{c}") for c in range(NC)]
        wu_in = [sem(f"wu_in{c}") for c in range(NC)]
        ad_in = sem("ad_in")
        wd_in = sem("wd_in")
        b_raw_in = [sem(f"b_raw_in{i}") for i in range(2)]
        bd_raw_in = [sem(f"bd_raw_in{i}") for i in range(2)]
        b_gate_hi_ready = sem("b_gate_hi_ready")
        b_gate_ready = sem("b_gate_ready")
        b_up_hi_ready = sem("b_up_hi_ready")
        b_up_ready = sem("b_up_ready")
        bd_hi_ready = sem("bd_hi_ready")
        bd_grp_ready = sem("bd_grp_ready")
        row_ready = sem("row_ready")
        consts_ready = sem("consts_ready")
        out_sent = [sem(f"out_sent{i}") for i in range(2)]
        dve_step = sem("dve_step")
        ident_step = sem("ident_step")
        ident_ready = sem("ident_ready")
        n_row_ready = sem("n_row_ready")
        diag_zeroed = sem("diag_zeroed")
        w0_own_ready = sem("w0_own_ready")
        diag_ready = sem("diag_ready")
        l0_done = sem("l0_done")
        x1_ready = sem("x1_ready")
        x1T_done = sem("x1T_done")
        x1T_ready = sem("x1T_ready")
        a_grp_ready = sem("a_grp_ready")
        a_done = sem("a_done")
        xa_ready = sem("xa_ready")
        xaT_done = sem("xaT_done")
        xaT_ready = sem("xaT_ready")
        split_hi = sem("split_hi")
        split_lo = sem("split_lo")
        xs_hi_ready = sem("xs_hi_ready")
        xs_lo_ready = sem("xs_lo_ready")
        ad_grp_ready = sem("ad_grp_ready")
        gate_done = sem("gate_done")
        up_done = sem("up_done")
        silu_ready = sem("silu_ready")
        h_ready = sem("h_ready")
        hT_done = sem("hT_done")
        hT_hi_ready = sem("hT_hi_ready")
        hT_lo_ready = sem("hT_lo_ready")
        down_done = sem("down_done")
        xd_ready = sem("xd_ready")
        xdT_done = sem("xdT_done")
        xd_hi_ready = sem("xd_hi_ready")
        xd_lo_ready = sem("xd_lo_ready")
        y_done = sem("y_done")
        out_ready = sem("out_ready")

        def w_chunk(mat, c, arrived):
            cols = slice(c * CH, (c + 1) * CH)
            return (w_raw[:, c, mat], w_hi[:, mat, :, cols], w_lo[:, mat, :, cols], (arrived, 16))

        WD = slice(LR, LR + D)
        splits = [
            w_chunk(0, 0, wg_in[0]),
            w_chunk(1, 0, wu_in[0]),
            w_chunk(0, 1, wg_in[1]),
            w_chunk(1, 1, wu_in[1]),
            (ad_raw[:], ad_hl[:, :, 0], ad_hl[:, :, 1], (ad_in, 16)),
            (wd_raw[:, 0], wdx[:, 0, 0:T, WD], wdx[:, 1, 0:T, WD], (wd_in, 16)),
            (wd_raw[:, 1], wdx[:, 0, T:KK, WD], wdx[:, 1, T:KK, WD], (wd_in, 16)),
        ]
        W_SPLIT, AD_SPLIT, WD_SPLIT = {(0, 0): 1, (1, 0): 2, (0, 1): 3, (1, 1): 4}, 5, (6, 7)
        SPLIT_AT = {5: [0], 6: [1], 9: [2], 10: [3, 4]}
        STEPS = G + 3
        B_AT, XS_AT = 7, 8

        def by_tile(ap):
            return ap.rearrange("q (p k) -> q k p", k=K)

        def rank_cols(g):
            return slice(0, LR) if g % 2 == 0 else slice(D, D + LR)

        def out_cols(g):
            return slice(LR, LR + D) if g % 2 == 0 else slice(0, D)

        tok = x.rearrange("(g s) c d -> (s c) g d", g=G)
        out_tok = out.rearrange("(g s) c d -> g (s c) d", g=G)

        block = ctx.enter_context(nc.Block())

        def load_x(eng, i):
            eng.dma_start(x_sb[:, 2 * i:2 * i + 2], tok[:, 2 * i:2 * i + 2]).then_inc(x_in[i], 16)

        def load_w(eng, c):
            for m, (W, arrived) in enumerate(((Wg, wg_in), (Wu, wu_in))):
                eng.dma_start(w_raw[:, c, m], W.rearrange("(p k) i -> p k i", k=K)[:, :, c * CH:(c + 1) * CH]
                              ).then_inc(arrived[c], 16)

        @block.sync
        def _(sp):
            sp.dma_start(idx_i[:], idx.partition_broadcast(P)).then_inc(idx_in, 16)
            sp.dma_start(w0_rep[:], w0).then_inc(w0_in, 16)
            for i in range(2, G // 2):
                load_x(sp, i)
            load_w(sp, 0)
            sp.wait_ge(idx_in, 16)

            def gather_b(g):
                _, ns = nc.values_load_multi_w_load_instructions(
                    idx_i[0:1, SG * g:SG * (g + 1)], engines=[ENG.SP], min_val=0, max_val=N - 1,
                    skip_runtime_bounds_check_because="adapter indices are 0..N-1")
                if g >= 2:
                    sp.wait_ge(b_up_ready, g - 1)
                for s in range(SG):
                    rows = B_all[bass.ds(ns[s], 1), :, 0:2 * I].rearrange("a r i -> (a r) i")
                    sp.dma_start(b_raw[s * C:(s + 1) * C, g % 2], rows).then_inc(b_raw_in[g % 2], 16)
                if g == 0:
                    load_w(sp, 1)
                    sp.dma_start(ad_raw[:], A_down).then_inc(ad_in, 16)
                    sp.dma_start(wd_raw[:].rearrange("p c t d -> p c (t d)"),
                                 Wd.rearrange("(c p t) d -> p c (t d)", c=NC, t=T)).then_inc(wd_in, 16)
                if g >= 2:
                    sp.wait_ge(bd_grp_ready, g - 1)
                for s in range(SG):
                    rows = B_all[bass.ds(ns[s], 1), :, 2 * I:BW].rearrange("a r i -> (a r) i")
                    sp.dma_start(bd_raw[s * C:(s + 1) * C, g % 2], rows).then_inc(bd_raw_in[g % 2], 16)

            def store(g):
                sp.wait_ge(out_ready, g + 1)
                sp.dma_start(out_tok[g], out_sb[:, g % 2]).then_inc(out_sent[g % 2], 16)

            gather_b(0)
            gather_b(1)
            for g in range(G):
                if g + 2 < G:
                    gather_b(g + 2)
                if g >= 2:
                    store(g - 2)
            store(G - 2)
            store(G - 1)
            for b in range(2):
                sp.wait_ge(out_sent[b], 16 * (G // 2))

        @block.gpsimd
        def _(pool):
            pool.memset(ident[:], 0.0).then_inc(ident_step, 1)
            pool.wait_ge(ident_step, 1)
            pool.affine_select(out=ident[:], in_=ident[:], compare_op=ALU.not_equal, fill=1.0, base=0,
                               pattern=[[-1, P]], channel_multiplier=1).then_inc(ident_ready, 1)
            pool.memset(w0_diag[:], 0.0).then_inc(diag_zeroed, 1)
            pool.iota(row[:], pattern=[[0, 1]], base=0, channel_multiplier=1).then_inc(row_ready, 1)

            pool.wait_ge(idx_in, 16)
            pool.wait_ge(a_in, 16)

            def adapters(g):
                _, ns = nc.values_load_multi_w_load_instructions(
                    idx_i[0:1, SG * g:SG * (g + 1)], engines=[ENG.Pool], min_val=0, max_val=N - 1,
                    skip_runtime_bounds_check_because="adapter indices are 0..N-1")
                return ns

            for g in range(G):
                ns = adapters(g)
                if g >= 2:
                    pool.wait_ge(a_done, g - 1)
                for s in range(SG):
                    last = pool.tensor_copy(
                        a_grp[:, g % 2, :, :, s, :],
                        a_raw[:, :, bass.ds(ns[s], 1), :, :].rearrange("p m a k r -> p k (m a) r"))
                last.then_inc(a_grp_ready, 1)
            pool.wait_ge(split_hi, AD_SPLIT)
            pool.wait_ge(split_lo, AD_SPLIT)
            for g in range(G):
                ns = adapters(g)
                at = 0 if g % 2 == 0 else LR + D
                if g >= 2:
                    pool.wait_ge(down_done, NC * (g - 1))
                for s in range(SG):
                    last = pool.tensor_copy(
                        wdx[:, :, :, at + s * R:at + (s + 1) * R].rearrange("p l t r -> p (l t) r"),
                        ad_hl[:, bass.ds(ns[s], 1)].rearrange("p a l t r -> p (a l t) r"))
                last.then_inc(ad_grp_ready, 1)

        @block.scalar
        def _(act):
            load_x(act, 0)
            act.dma_start(a_raw[:], A_in).then_inc(a_in, 16)
            load_x(act, 1)
            act.wait_ge(n_row_ready, 1)
            act.activation(act_warm[:], n_row[:, 0:1], ACT.Silu)

            act.wait_ge(diag_zeroed, 1)
            for i in range(G // 2):
                act.wait_ge(w0_own_ready, i + 1)
                gs = slice(2 * i, 2 * i + 2)
                for s in range(SG):
                    rows = slice(s * C, (s + 1) * C)
                    last = act.activation(w0_diag[rows, gs, s, :], w0_own[rows, gs, :], ACT.Copy)
                last.then_inc(diag_ready, 1)

            def x1T_out(g):
                act.wait_ge(x1T_done, g + 1)
                act.activation(xT[:, g, 0:K], x1T_ps[g % 2][:, 0:K * P].rearrange("p (k t) -> p k t", k=K),
                               ACT.Copy).then_inc(x1T_ready, 1)

            def xaT_out(g):
                act.wait_ge(xaT_done, g + 1)
                act.activation(xT[:, g, K:K + 2], xaT_ps[g % 2][:, 0:2 * P].rearrange("p (m t) -> p m t", m=2),
                               ACT.Copy).then_inc(xaT_ready, 1)

            def weight_hi(i):
                raw, hi, _, (arrived, count) = splits[i]
                act.wait_ge(arrived, count)
                act.activation(hi, raw, ACT.Copy).then_inc(split_hi, 1)

            def group_hi(g):
                act.wait_ge(x1T_ready, g + 1)
                act.wait_ge(xaT_ready, g + 1)
                if g >= 2:
                    act.wait_ge(up_done, NC * (g - 1))
                act.activation(xs_hi[:, g % 2], xT[:, g], ACT.Copy).then_inc(xs_hi_ready, 1)

            def b_hi(g, mat):
                act.wait_ge(b_raw_in[g % 2], 16 * SG * (g // 2 + 1))
                if g == 0:
                    act.wait_ge(consts_ready, 2)
                if g >= 2:
                    act.wait_ge((gate_done, up_done)[mat], NC * (g - 1))
                cols = slice(mat * I, (mat + 1) * I)
                act.activation(b_grp[:, g % 2, cols], b_raw[:, g % 2, cols], ACT.Copy, scale=sign_lo[:]
                               ).then_inc((b_gate_hi_ready, b_up_hi_ready)[mat], 1)

            def bd_hi(g):
                act.wait_ge(bd_raw_in[g % 2], 16 * SG * (g // 2 + 1))
                if g >= 2:
                    act.wait_ge(y_done, g - 1)
                act.activation(bd_grp[:, g % 2], bd_raw[:, g % 2], ACT.Copy, scale=sign_lo[:]).then_inc(bd_hi_ready, 1)

            for t in range(STEPS):
                if 1 <= t <= G:
                    x1T_out(t - 1)
                if 3 <= t:
                    xaT_out(t - 3)
                if t == B_AT:
                    b_hi(0, 0)
                    b_hi(0, 1)
                if t == XS_AT:
                    group_hi(0)
                for i in SPLIT_AT.get(t, []):
                    weight_hi(i)

            def silu(q):
                act.wait_ge(gate_done, q + 1)
                if q >= 2:
                    act.wait_ge(h_ready, q - 1)
                act.activation(sg[:, q % 2], gate_ps[q % 2][:], ACT.Silu).then_inc(silu_ready, 1)

            def hidden_hi(q):
                act.wait_ge(hT_done, q + 1)
                if q >= 2:
                    act.wait_ge(down_done, q - 1)
                act.activation(hT_hi[:, q % 2], hT_ps[:].rearrange("p (t n) -> p t n", t=T),
                               ACT.Copy).then_inc(hT_hi_ready, 1)

            def rank_hi(g):
                act.wait_ge(xdT_done, g + 1)
                if g >= 1:
                    act.wait_ge(y_done, g)
                act.activation(xd_hi[:], xdT_ps[:, 0:P], ACT.Copy).then_inc(xd_hi_ready, 1)

            for q in range(Q + 1):
                g, c = q // NC, q % NC
                if q < Q:
                    silu(q)
                if q >= 1:
                    hidden_hi(q - 1)
                if c == 0 and g + 1 < G:
                    group_hi(g + 1)
                if c == 1 and g >= 1:
                    rank_hi(g - 1)
                if q == 0:
                    weight_hi(5)
                if q == 1:
                    weight_hi(6)
                    bd_hi(0)
                if q < Q and g + 1 < G:
                    b_hi(g + 1, c)
                if c == 1 and g + 1 < G:
                    bd_hi(g + 1)
            rank_hi(G - 1)

        @block.tensor
        def _(pe):
            def l0(g):
                if g % 2 == 0:
                    pe.wait_ge(diag_ready, g // 2 + 1)
                    pe.wait_ge(x_in[g // 2], 16)
                if g >= 2:
                    pe.wait_ge(x1_ready, g - 1)
                pe.matmul(l0_ps[g % 2][:, 0:D], w0_diag[:, g].rearrange("p s c -> p (s c)"), x_sb[:, g],
                          start=True, stop=True).then_inc(l0_done, 1)

            def x1_turn(g):
                if g == 0:
                    pe.wait_ge(ident_ready, 1)
                pe.wait_ge(x1_ready, g + 1)
                if g >= 2:
                    pe.wait_ge(x1T_ready, g - 1)
                for k in range(K):
                    mm = pe.transpose(x1T_ps[g % 2][:, k * P:(k + 1) * P], x1[:, g, k], ident[:])
                mm.then_inc(x1T_done, 1)

            def rank_in(g):
                pe.wait_ge(x1T_ready, g + 1)
                pe.wait_ge(a_grp_ready, g + 1)
                if g >= 2:
                    pe.wait_ge(xa_ready, g - 1)
                for k in range(K):
                    mm = pe.matmul(a_ps[g % 2][:, 0:2 * LR], xT[:, g, k],
                                   a_grp[:, g % 2, k].rearrange("p m s r -> p (m s r)"),
                                   start=(k == 0), stop=(k == K - 1))
                mm.then_inc(a_done, 1)

            def xa_turn(g):
                pe.wait_ge(xa_ready, g + 1)
                if g >= 2:
                    pe.wait_ge(xaT_ready, g - 1)
                for m in range(2):
                    mm = pe.transpose(xaT_ps[g % 2][:, m * P:(m + 1) * P],
                                      xa[:, g % 2, m].rearrange("p s l r -> p (s l r)"), ident[:])
                mm.then_inc(xaT_done, 1)

            for t in range(STEPS):
                if t < G:
                    l0(t)
                if 1 <= t <= G:
                    x1_turn(t - 1)
                if 2 <= t <= G + 1:
                    rank_in(t - 2)
                if 3 <= t:
                    xa_turn(t - 3)

            def half_mlp(q, mat, ps, done):
                g, c = q // NC, q % NC
                cols = slice(c * CH, (c + 1) * CH)
                b = g % 2
                if g == 0:
                    pe.wait_ge(split_hi, W_SPLIT[mat, c])
                    pe.wait_ge(split_lo, W_SPLIT[mat, c])
                for k in range(K):
                    pe.matmul(ps, xs_hi[:, b, k], w_hi[:, mat, k, cols], start=(k == 0), stop=False)
                    pe.matmul(ps, xs_hi[:, b, k], w_lo[:, mat, k, cols], start=False, stop=False)
                    pe.matmul(ps, xs_lo[:, b, k], w_hi[:, mat, k, cols], start=False, stop=False)
                if c == 0 and mat == 0:
                    pe.wait_ge(b_gate_ready, g + 1)
                if c == 0 and mat == 1:
                    pe.wait_ge(b_up_ready, g + 1)
                rows = b_grp[:, b, mat * I + c * CH:mat * I + (c + 1) * CH]
                pe.matmul(ps, xs_hi[:, b, K + mat], rows, start=False, stop=False)
                pe.matmul(ps, xs_lo[:, b, K + mat], rows, start=False, stop=True).then_inc(done, 1)

            def gate(q):
                g, c = q // NC, q % NC
                if c == 0:
                    pe.wait_ge(xs_hi_ready, g + 1)
                    pe.wait_ge(xs_lo_ready, g + 1)
                if q >= 2:
                    pe.wait_ge(silu_ready, q - 1)
                half_mlp(q, 0, gate_ps[q % 2][:], gate_done)

            def up(q):
                if q >= 2:
                    pe.wait_ge(h_ready, q - 1)
                half_mlp(q, 1, up_ps[q % 2][:], up_done)

            def hidden_turn(q):
                pe.wait_ge(h_ready, q + 1)
                if q == 0:
                    pe.wait_ge(xaT_ready, G)
                else:
                    pe.wait_ge(hT_hi_ready, q)
                    pe.wait_ge(hT_lo_ready, q)
                for t in range(T):
                    mm = pe.transpose(hT_ps[:, t * P:(t + 1) * P], h[:, q % 2, t], ident[:])
                mm.then_inc(hT_done, 1)

            def down(q):
                g, c = q // NC, q % NC
                if c == 0:
                    pe.wait_ge(ad_grp_ready, g + 1)
                    if g >= 2:
                        pe.wait_ge(out_ready, g - 1)
                if g == 0:
                    pe.wait_ge(split_hi, WD_SPLIT[c])
                    pe.wait_ge(split_lo, WD_SPLIT[c])
                pe.wait_ge(hT_hi_ready, q + 1)
                pe.wait_ge(hT_lo_ready, q + 1)
                at = 0 if g % 2 == 0 else LR
                ps = y_ps[g % 2][:, 0:LR + D]
                for t in range(T):
                    kk = c * T + t
                    hi, lo = (wdx[:, l, kk, at:at + LR + D] for l in range(2))
                    pe.matmul(ps, hT_hi[:, q % 2, t], hi, start=(kk == 0), stop=False)
                    pe.matmul(ps, hT_hi[:, q % 2, t], lo, start=False, stop=False)
                    mm = pe.matmul(ps, hT_lo[:, q % 2, t], hi, start=False, stop=(kk == KK - 1))
                mm.then_inc(down_done, 1)

            def rank_turn(g):
                pe.wait_ge(xd_ready, g + 1)
                if g >= 1:
                    pe.wait_ge(xd_hi_ready, g)
                    pe.wait_ge(xd_lo_ready, g)
                pe.transpose(xdT_ps[:, 0:P], xd[:].rearrange("p s l r -> p (s l r)"), ident[:]).then_inc(xdT_done, 1)

            def rank_out(g):
                pe.wait_ge(bd_grp_ready, g + 1)
                pe.wait_ge(xd_hi_ready, g + 1)
                pe.wait_ge(xd_lo_ready, g + 1)
                ps = y_ps[g % 2][:, out_cols(g)]
                pe.matmul(ps, xd_hi[:], bd_grp[:, g % 2], start=False, stop=False, skip_group_check=True)
                pe.matmul(ps, xd_lo[:], bd_grp[:, g % 2], start=False, stop=True,
                          skip_group_check=True).then_inc(y_done, 1)

            for q in range(Q + 1):
                g, c = q // NC, q % NC
                if q < Q:
                    gate(q)
                if q >= 1:
                    hidden_turn(q - 1)
                if c == 1 and g >= 1:
                    rank_turn(g - 1)
                if q < Q:
                    up(q)
                if c == 1 and g >= 1:
                    rank_out(g - 1)
                if q >= 1:
                    down(q - 1)
            rank_turn(G - 1)
            rank_out(G - 1)

        @block.vector
        def _(dve):
            steps = 0

            def chain(ins):
                nonlocal steps
                steps += 1
                ins.then_inc(dve_step, 1)
                dve.wait_ge(dve_step, steps)

            for n in range(N):
                last = dve.memset(n_row[:, n:n + 1], float(n))
            last.then_inc(n_row_ready, 1)
            chain(dve.memset(own[:], 0.0))
            for s in range(SG):
                last = dve.memset(own[s * C:(s + 1) * C, s:2 * SG:SG], 1.0)
            chain(last)
            dve.wait_ge(idx_in, 16)
            chain(dve.tensor_copy(idx_f[:].rearrange("p g s -> p (g s)"), idx_i[:]))
            own_g = own[:, 0:SG].unsqueeze(1).to_broadcast([P, G, SG])
            chain(dve.tensor_tensor(idx_sel[:], idx_f[:], own_g, ALU.mult))
            chain(dve.tensor_reduce(idx_own[:], idx_sel[:], AX.X, ALU.add))
            chain(dve.tensor_tensor(onehot[:], idx_own[:].unsqueeze(2).to_broadcast([P, G, N]),
                                    n_row[:].unsqueeze(1).to_broadcast([P, G, N]), ALU.is_equal))
            dve.wait_ge(row_ready, 1)
            chain(dve.tensor_scalar(row_bit[:], row[:], R, None, ALU.bitwise_and))
            dve.tensor_scalar(is_lo[:], row_bit[:], 1.0 / R, None, ALU.mult).then_inc(consts_ready, 1)
            dve.tensor_scalar(sign_lo[:], row_bit[:], -2.0 / R, 1.0, ALU.mult, ALU.add).then_inc(consts_ready, 1)
            dve.wait_ge(w0_in, 16)

            def own_weights(i):
                prod = w0_prod[:, i % 2].rearrange("p (g c n) -> p g c n", g=2, c=C)
                if i >= 2:
                    dve.wait_ge(w0_own_ready, i - 1)
                for j in range(2):
                    last = dve.tensor_tensor(
                        prod[:, j], w0_rep[:],
                        onehot[:, 2 * i + j].unsqueeze(1).to_broadcast([P, C, N]), ALU.mult)
                chain(last)
                dve.tensor_reduce(w0_own[:, 2 * i:2 * i + 2], prod, AX.X, ALU.add).then_inc(w0_own_ready, 1)

            def x1_add(g):
                dve.wait_ge(l0_done, g + 1)
                dve.tensor_tensor(x1[:, g], by_tile(l0_ps[g % 2][:, 0:D]), by_tile(x_sb[:, g]),
                                  ALU.add).then_inc(x1_ready, 1)

            def xa_place(g):
                dve.wait_ge(a_done, g + 1)
                if g >= 2:
                    dve.wait_ge(xaT_done, g - 1)
                dve.tensor_tensor(
                    xa[:, g % 2].rearrange("p m s l r -> p (m s) l r"),
                    a_ps[g % 2][:, 0:2 * LR].rearrange("p (j r) -> p j r", r=R).unsqueeze(2)
                    .to_broadcast([P, 2 * SG, 2, R]),
                    own[:].unsqueeze(2).unsqueeze(3).to_broadcast([P, 2 * SG, 2, R]), ALU.mult).then_inc(xa_ready, 1)

            def weight_lo(i):
                raw, hi, lo, _ = splits[i]
                dve.wait_ge(split_hi, i + 1)
                dve.tensor_tensor(lo, raw, hi.bitcast(F32), ALU.subtract).then_inc(split_lo, 1)

            def b_lo(g, mat):
                dve.wait_ge((b_gate_hi_ready, b_up_hi_ready)[mat], g + 1)
                rows = b_grp[:, g % 2, mat * I:(mat + 1) * I]
                dve.scalar_tensor_tensor(out=rows, in0=b_raw[:, g % 2, mat * I:(mat + 1) * I], scalar=is_lo[:],
                                         in1=rows.bitcast(F32), op0=ALU.mult, op1=ALU.add
                                         ).then_inc((b_gate_ready, b_up_ready)[mat], 1)

            def bd_lo(g):
                dve.wait_ge(bd_hi_ready, g + 1)
                dve.scalar_tensor_tensor(out=bd_grp[:, g % 2], in0=bd_raw[:, g % 2], scalar=is_lo[:],
                                         in1=bd_grp[:, g % 2].bitcast(F32), op0=ALU.mult, op1=ALU.add
                                         ).then_inc(bd_grp_ready, 1)

            def group_lo(g):
                dve.wait_ge(xs_hi_ready, g + 1)
                dve.tensor_tensor(xs_lo[:, g % 2], xT[:, g], xs_hi[:, g % 2].bitcast(F32),
                                  ALU.subtract).then_inc(xs_lo_ready, 1)

            own_weights(0)
            own_weights(1)
            for t in range(STEPS):
                if t < G:
                    x1_add(t)
                if t in (0, 2):
                    own_weights(2 + t // 2)
                if 2 <= t <= G + 1:
                    xa_place(t - 2)
                if t == B_AT:
                    b_lo(0, 0)
                    b_lo(0, 1)
                if t == XS_AT:
                    group_lo(0)
                for i in SPLIT_AT.get(t, []):
                    weight_lo(i)

            def hidden_lo(q):
                dve.wait_ge(hT_hi_ready, q + 1)
                dve.tensor_tensor(hT_lo[:, q % 2], hT_ps[:].rearrange("p (t n) -> p t n", t=T),
                                  hT_hi[:, q % 2].bitcast(F32), ALU.subtract).then_inc(hT_lo_ready, 1)

            def hidden(q):
                dve.wait_ge(silu_ready, q + 1)
                dve.wait_ge(up_done, q + 1)
                if q >= 2:
                    dve.wait_ge(hT_done, q - 1)
                dve.tensor_tensor(h[:, q % 2], up_ps[q % 2][:].rearrange("n (p t) -> n t p", t=T),
                                  sg[:, q % 2].rearrange("n (p t) -> n t p", t=T), ALU.mult).then_inc(h_ready, 1)

            def rank_place(g):
                dve.wait_ge(down_done, NC * (g + 1))
                if g >= 1:
                    dve.wait_ge(xdT_done, g)
                dve.tensor_tensor(
                    xd[:], y_ps[g % 2][:, rank_cols(g)].rearrange("p (s r) -> p s r", s=SG).unsqueeze(2)
                    .to_broadcast([P, SG, 2, R]),
                    own[:, 0:SG].unsqueeze(2).unsqueeze(3).to_broadcast([P, SG, 2, R]), ALU.mult).then_inc(xd_ready, 1)

            def rank_lo(g):
                dve.wait_ge(xd_hi_ready, g + 1)
                dve.tensor_tensor(xd_lo[:], xdT_ps[:, 0:P], xd_hi[:].bitcast(F32), ALU.subtract).then_inc(xd_lo_ready, 1)

            def final(g):
                dve.wait_ge(y_done, g + 1)
                if g >= 2:
                    dve.wait_ge(out_sent[g % 2], 16 * (g // 2))
                dve.tensor_tensor(by_tile(out_sb[:, g % 2]), by_tile(y_ps[g % 2][:, out_cols(g)]), x1[:, g],
                                  ALU.add).then_inc(out_ready, 1)

            for q in range(Q + 1):
                g, c = q // NC, q % NC
                if c == 1 and g >= 1:
                    rank_place(g - 1)
                if q >= 1:
                    hidden_lo(q - 1)
                if c == 1 and g >= 1:
                    rank_lo(g - 1)
                if q < Q:
                    hidden(q)
                if c == 1 and g >= 1:
                    final(g - 1)
                if c == 0 and g + 1 < G:
                    group_lo(g + 1)
                if q == 0:
                    weight_lo(5)
                if q == 1:
                    weight_lo(6)
                    bd_lo(0)
                if q < Q and g + 1 < G:
                    b_lo(g + 1, c)
                if c == 1 and g + 1 < G:
                    bd_lo(g + 1)
            rank_place(G - 1)
            rank_lo(G - 1)
            final(G - 1)


def kernel(x, itok_B_0_7, L0_cond_weights, L1_cond_Wg, L1_cond_Wu, L1_cond_Wd, L1_cond_Ag, L1_cond_Bg,
           L1_cond_Au, L1_cond_Bu, L1_cond_Ad, L1_cond_Bd):
    import numpy as _np
    import concourse.bacc as _bacc
    from concourse import mybir as _mybir
    from concourse.bass_utils import run_bass_kernel_spmd as _run

    P, T = 128, 4
    N, D, R = L1_cond_Ag.shape
    I = L1_cond_Ad.shape[1]
    a_in = _np.stack([L1_cond_Ag, L1_cond_Au]).reshape(2, N, P, D // P, R).transpose(2, 0, 1, 3, 4)
    a_down = _np.reshape(L1_cond_Ad, (N, I // (P * T), P, T, R)).transpose(2, 0, 1, 3, 4).reshape(P, N, I // P, R)
    w0 = _np.transpose(L0_cond_weights, (1, 2, 0))
    C = w0.shape[0]
    b_all = _np.concatenate([L1_cond_Bg, L1_cond_Bu, L1_cond_Bd], axis=2)
    data = {
        "x": x, "idx": itok_B_0_7, "w0": _np.concatenate([w0] * (P // C)),
        "Wg": L1_cond_Wg, "Wu": L1_cond_Wu, "Wd": L1_cond_Wd, "A_in": a_in,
        "B_all": _np.concatenate([b_all, b_all], axis=1), "A_down": a_down,
    }
    nc = _bacc.Bacc("TRN2", target_bir_lowering=False, num_devices=1)
    arrays, args = {}, []
    for name, a in data.items():
        a = _np.ascontiguousarray(a)
        arrays[f"in_{name}"] = a
        args.append(nc.dram_tensor(f"in_{name}", a.shape, _mybir.dt.from_np(a.dtype), kind="ExternalInput").ap())
    args.append(nc.dram_tensor("out_dram", x.shape, _mybir.dt.float32, kind="ExternalOutput").ap())
    cond_resid_kernel(nc, *args)
    r = _run(nc, [arrays], core_ids=[0])
    return r.results[0]["out_dram"]
```

```python
from contextlib import ExitStack

import concourse.bass as bass
from concourse import mybir

F32 = mybir.dt.float32
F32R = mybir.dt.float32r
I32 = mybir.dt.int32
ALU = mybir.AluOpType
ACT = mybir.ActivationFunctionType
ENG = mybir.EngineType


def cond_resid_kernel(nc, x, idx, w0, Wg, Wu, Wd, A_in, B_all, A_down, out):
    S, C, D = x.shape
    N, R2, BW = B_all.shape
    R = R2 // 2
    I = Wg.shape[1]
    P = 128
    SG = P // C
    G = S // SG
    K = D // P
    CH = 512
    NC = I // CH
    T = CH // P
    KK = NC * T
    Q = G * NC
    LR = SG * R
    WX = 2 * LR + D
    WARM = 9
    assert 2 * LR == P and SG * C == P and 2 * R == C and BW == 2 * I + D

    with ExitStack() as ctx:
        def sb(name, shape, dt=F32):
            return ctx.enter_context(nc.sbuf_tensor(name, shape, dt))

        def sem(name):
            return ctx.enter_context(nc.semaphore(name))

        def bank(name):
            return ctx.enter_context(nc.psum_tensor(name, [P, 512], F32))

        idx_i = sb("idx_i", [P, S], I32)
        own = sb("own", [P, 2 * SG])
        act_warm = sb("act_warm", [P, 1])
        ident = sb("ident", [P, P])
        w0_rep = sb("w0_rep", [P, N, C])
        w0_own = sb("w0_own", [P, G, SG, C])
        pe_warm = sb("pe_warm", [P, P])
        w0_diag = sb("w0_diag", [P, G, SG, C])
        x_sb = sb("x_sb", [P, G, D])
        x1 = sb("x1", [P, G, K, P])
        xT = sb("xT", [P, G, 4, P])
        xs_hi = sb("xs_hi", [P, 2, 4, P], F32R)
        xs_lo = sb("xs_lo", [P, 2, 4, P], F32R)
        a_raw = sb("a_raw", [P, 2, N, K, R])
        a_grp = sb("a_grp", [P, 2, K, 2, SG, R])
        xa = sb("xa", [P, 2, 2, SG, 2, R])
        w_raw = sb("w_raw", [P, NC, 2, K, CH])
        w_hi = sb("w_hi", [P, 2, K, I], F32R)
        w_lo = sb("w_lo", [P, 2, K, I], F32R)
        row = sb("row", [P, 1], I32)
        row_bit = sb("row_bit", [P, 1], I32)
        is_lo = sb("is_lo", [P, 1])
        sign_lo = sb("sign_lo", [P, 1])
        b_raw = sb("b_raw", [P, 2, 2 * I])
        bd_raw = sb("bd_raw", [P, 2, D])
        b_grp = sb("b_grp", [P, 2, 2 * I], F32R)
        bd_grp = sb("bd_grp", [P, 2, D], F32R)
        ad_raw = sb("ad_raw", [P, N, KK, R])
        ad_grp = sb("ad_grp", [P, 2, KK, SG, R])
        wd_raw = sb("wd_raw", [P, NC, T, D])
        wdx = sb("wdx", [P, 2, KK, WX], F32R)
        sg = sb("sg", [P, 2, CH])
        h = sb("h", [P, 2, T, P])
        hT_hi = sb("hT_hi", [P, 2, T, P], F32R)
        hT_lo = sb("hT_lo", [P, 2, T, P], F32R)
        xd = sb("xd", [P, SG, 2, R])
        xd_hi = sb("xd_hi", [P, P], F32R)
        xd_lo = sb("xd_lo", [P, P], F32R)
        out_sb = sb("out_sb", [P, 2, D])
        gate_ps = [bank(f"gate_ps{i}") for i in range(2)]
        up_ps = [bank(f"up_ps{i}") for i in range(2)]
        y_ps = [bank(f"y_ps{i}") for i in range(2)]
        hT_ps = bank("hT_ps")
        side_ps = bank("side_ps")

        def l0_at(g):
            return (gate_ps[g] if g < 2 else side_ps)[:, 0:D]

        def x1T_at(g):
            return (up_ps[g] if g < 2 else side_ps)[:, D:D + K * P]

        def a_at(g):
            return (y_ps[g] if g < 2 else side_ps)[:, 0:2 * LR]

        def xaT_at(g):
            return (hT_ps, y_ps[1], side_ps)[min(g, 2)][:, D:D + 2 * P]

        last_y = gate_ps[0][:, 0:D]

        idx_in = sem("idx_in")
        w0_in = sem("w0_in")
        x_in = [sem(f"x_in{i}") for i in range(G // 2)]
        a_in = sem("a_in")
        wg_in = [sem(f"wg_in{c}") for c in range(NC)]
        wu_in = [sem(f"wu_in{c}") for c in range(NC)]
        ad_in = sem("ad_in")
        wd_in = [sem(f"wd_in{c}") for c in range(NC)]
        b_raw_in = [[sem(f"b_raw_in{i}_{c}") for c in range(NC)] for i in range(2)]
        bd_raw_in = [sem(f"bd_raw_in{i}") for i in range(2)]
        b_hi_ready = sem("b_hi_ready")
        b_ready = sem("b_ready")
        bd_hi_ready = sem("bd_hi_ready")
        bd_grp_ready = sem("bd_grp_ready")
        row_ready = sem("row_ready")
        consts_ready = sem("consts_ready")
        out_sent = [sem(f"out_sent{i}") for i in range(2)]
        dve_step = sem("dve_step")
        ident_step = sem("ident_step")
        ident_ready = sem("ident_ready")
        warm_ready = sem("warm_ready")
        own_ready = sem("own_ready")
        w0_own_ready = sem("w0_own_ready")
        diag_ready = sem("diag_ready")
        l0_done = sem("l0_done")
        x1_ready = sem("x1_ready")
        x1T_done = sem("x1T_done")
        x1T_ready = sem("x1T_ready")
        a_grp_ready = sem("a_grp_ready")
        a_done = sem("a_done")
        xa_ready = sem("xa_ready")
        xaT_done = sem("xaT_done")
        xaT_ready = sem("xaT_ready")
        split_hi = sem("split_hi")
        split_lo = sem("split_lo")
        xs_hi_ready = sem("xs_hi_ready")
        xs_lo_ready = sem("xs_lo_ready")
        x1_hi_ready = sem("x1_hi_ready")
        x1_lo_ready = sem("x1_lo_ready")
        ad_grp_ready = sem("ad_grp_ready")
        ad_hi_ready = sem("ad_hi_ready")
        ad_lo_ready = sem("ad_lo_ready")
        gate_done = sem("gate_done")
        up_done = sem("up_done")
        silu_ready = sem("silu_ready")
        h_ready = sem("h_ready")
        hT_done = sem("hT_done")
        hT_hi_ready = sem("hT_hi_ready")
        hT_lo_ready = sem("hT_lo_ready")
        down_done = sem("down_done")
        last_rank_done = sem("last_rank_done")
        last_sum_ready = sem("last_sum_ready")
        xd_ready = sem("xd_ready")
        xdT_done = sem("xdT_done")
        xd_hi_ready = sem("xd_hi_ready")
        xd_lo_ready = sem("xd_lo_ready")
        y_done = sem("y_done")
        out_ready = sem("out_ready")

        def w_chunk(mat, c, arrived):
            cols = slice(c * CH, (c + 1) * CH)
            return (w_raw[:, c, mat], w_hi[:, mat, :, cols], w_lo[:, mat, :, cols], (arrived, 16))

        def b_part(tile, c):
            return tile.rearrange("p (m i) -> p m i", m=2)[:, :, c * CH:(c + 1) * CH]

        WD = slice(LR, LR + D)
        splits = [
            w_chunk(0, 0, wg_in[0]),
            w_chunk(1, 0, wu_in[0]),
            w_chunk(0, 1, wg_in[1]),
            w_chunk(1, 1, wu_in[1]),
            (wd_raw[:, 0], wdx[:, 0, 0:T, WD], wdx[:, 1, 0:T, WD], (wd_in[0], 16)),
            (wd_raw[:, 1], wdx[:, 0, T:KK, WD], wdx[:, 1, T:KK, WD], (wd_in[1], 16)),
        ]
        W_SPLIT, WD_SPLIT = {(0, 0): 1, (1, 0): 2, (0, 1): 3, (1, 1): 4}, (5, 6)

        def by_tile(ap):
            return ap.rearrange("q (p k) -> q k p", k=K)

        def hidden_parts(q):
            return [slice(0, T // 2), slice(T // 2, T)] if q == Q - 1 else [slice(0, T)]

        def hT_at(q, ts):
            ps = up_ps[0] if q == Q - 1 and ts.start > 0 else hT_ps
            return ps.rearrange("p (t n) -> p t n", t=T)[:, ts]

        def ad_cols(g):
            return slice(0, LR) if g % 2 == 0 else slice(LR + D, WX)

        def rank_cols(g):
            return slice(0, LR) if g % 2 == 0 else slice(D, D + LR)

        def out_cols(g):
            return slice(LR, LR + D) if g % 2 == 0 else slice(0, D)

        tok = x.rearrange("(g s) c d -> (s c) g d", g=G)
        out_tok = out.rearrange("(g s) c d -> g (s c) d", g=G)

        block = ctx.enter_context(nc.Block())

        def load_x(eng, i):
            eng.dma_start(x_sb[:, 2 * i:2 * i + 2], tok[:, 2 * i:2 * i + 2]).then_inc(x_in[i], 16)

        def load_w(eng, c):
            for m, (W, arrived) in enumerate(((Wg, wg_in), (Wu, wu_in))):
                eng.dma_start(w_raw[:, c, m], W.rearrange("(p k) i -> p k i", k=K)[:, :, c * CH:(c + 1) * CH]
                              ).then_inc(arrived[c], 16)

        @block.sync
        def _(sp):
            sp.dma_start(idx_i[:], idx.partition_broadcast(P)).then_inc(idx_in, 16)
            load_x(sp, 0)
            load_w(sp, 0)
            sp.wait_ge(idx_in, 16)

            def samples(g):
                _, ns = nc.values_load_multi_w_load_instructions(
                    idx_i[0:1, SG * g:SG * (g + 1)], engines=[ENG.SP], min_val=0, max_val=N - 1,
                    skip_runtime_bounds_check_because="adapter indices are 0..N-1")
                return ns

            def gather_b(g, c, ns):
                if g >= 2:
                    sp.wait_ge(b_ready, NC * (g - 2) + c + 1)
                for s in range(SG):
                    rows = b_part(B_all[bass.ds(ns[s], 1), :, 0:2 * I].rearrange("a r i -> (a r) i"), c)
                    sp.dma_start(b_part(b_raw[s * C:(s + 1) * C, g % 2], c), rows).then_inc(b_raw_in[g % 2][c], 16)

            def gather_bd(g, ns):
                if g >= 2:
                    sp.wait_ge(bd_grp_ready, g - 1)
                for s in range(SG):
                    rows = B_all[bass.ds(ns[s], 1), :, 2 * I:BW].rearrange("a r i -> (a r) i")
                    sp.dma_start(bd_raw[s * C:(s + 1) * C, g % 2], rows).then_inc(bd_raw_in[g % 2], 16)

            def load_wd(c):
                sp.dma_start(wd_raw[:, c].rearrange("p t d -> p (t d)"),
                             Wd.rearrange("(c p t) d -> c p (t d)", c=NC, t=T)[c]).then_inc(wd_in[c], 16)

            def store(g):
                sp.wait_ge(out_ready, g + 1)
                sp.dma_start(out_tok[g], out_sb[:, g % 2]).then_inc(out_sent[g % 2], 16)

            ns = samples(0)
            gather_b(0, 0, ns)
            load_x(sp, 1)
            load_w(sp, 1)
            gather_b(0, 1, ns)
            sp.dma_start(ad_raw[:], A_down).then_inc(ad_in, 16)
            load_wd(0)
            gather_bd(0, ns)
            ns = samples(1)
            gather_b(1, 0, ns)
            load_wd(1)
            gather_b(1, 1, ns)
            gather_bd(1, ns)
            for i in range(2, G // 2):
                load_x(sp, i)
            for g in range(G):
                if g + 2 < G:
                    ns = samples(g + 2)
                    for c in range(NC):
                        gather_b(g + 2, c, ns)
                    gather_bd(g + 2, ns)
                if g >= 2:
                    store(g - 2)
            store(G - 2)
            store(G - 1)
            for b in range(2):
                sp.wait_ge(out_sent[b], 16 * (G // 2))

        @block.gpsimd
        def _(pool):
            pool.memset(ident[:], 0.0).then_inc(ident_step, 1)
            pool.wait_ge(ident_step, 1)
            pool.affine_select(out=ident[:], in_=ident[:], compare_op=ALU.not_equal, fill=1.0, base=0,
                               pattern=[[-1, P]], channel_multiplier=1).then_inc(ident_ready, 1)
            pool.iota(row[:], pattern=[[0, 1]], base=0, channel_multiplier=1).then_inc(row_ready, 1)

            pool.wait_ge(idx_in, 16)

            def adapters(g):
                _, ns = nc.values_load_multi_w_load_instructions(
                    idx_i[0:1, SG * g:SG * (g + 1)], engines=[ENG.Pool], min_val=0, max_val=N - 1,
                    skip_runtime_bounds_check_because="adapter indices are 0..N-1")
                return ns

            def gather_w0(g, ns):
                if g == 0:
                    pool.wait_ge(w0_in, 16)
                for s in range(SG):
                    last = pool.tensor_copy(w0_own[:, g, s, :],
                                            w0_rep[:, bass.ds(ns[s], 1), :].rearrange("p a c -> p (a c)"))
                last.then_inc(w0_own_ready, 1)

            def gather_a(g, ns):
                if g == 0:
                    pool.wait_ge(a_in, 16)
                if g >= 2:
                    pool.wait_ge(a_done, g - 1)
                for s in range(SG):
                    last = pool.tensor_copy(
                        a_grp[:, g % 2, :, :, s, :],
                        a_raw[:, :, bass.ds(ns[s], 1), :, :].rearrange("p m a k r -> p k (m a) r"))
                last.then_inc(a_grp_ready, 1)

            def gather_ad(g, ns):
                if g == 0:
                    pool.wait_ge(ad_in, 16)
                if g >= 2:
                    pool.wait_ge(ad_lo_ready, g - 1)
                for s in range(SG):
                    last = pool.tensor_copy(
                        ad_grp[:, g % 2, :, s, :],
                        ad_raw[:, bass.ds(ns[s], 1)].rearrange("p a t r -> p (a t) r"))
                last.then_inc(ad_grp_ready, 1)

            first_ns = [adapters(g) for g in range(2)]
            for g in range(2):
                gather_w0(g, first_ns[g])
            for g in range(2):
                gather_a(g, first_ns[g])
            ns = adapters(2)
            gather_w0(2, ns)
            gather_a(2, ns)
            for g in range(G):
                gather_ad(g, adapters(g))
                if g + 3 < G:
                    ns = adapters(g + 3)
                    gather_w0(g + 3, ns)
                    gather_a(g + 3, ns)

        @block.scalar
        def _(act):
            act.dma_start(w0_rep[:], w0).then_inc(w0_in, 16)
            act.dma_start(a_raw[:], A_in).then_inc(a_in, 16)
            act.wait_ge(warm_ready, 1)
            act.activation(act_warm[:], pe_warm[:, 0:1], ACT.Silu)

            def x1T_out(g):
                act.wait_ge(x1T_done, g + 1)
                act.activation(xT[:, g, 0:K], x1T_at(g).rearrange("p (k t) -> p k t", k=K),
                               ACT.Copy).then_inc(x1T_ready, 1)

            def xaT_out(g):
                act.wait_ge(xaT_done, g + 1)
                act.activation(xT[:, g, K:K + 2], xaT_at(g).rearrange("p (m t) -> p m t", m=2),
                               ACT.Copy).then_inc(xaT_ready, 1)

            def weight_hi(i):
                raw, hi, _, (arrived, count) = splits[i]
                act.wait_ge(arrived, count)
                act.activation(hi, raw, ACT.Copy).then_inc(split_hi, 1)

            def x1_hi_first():
                act.wait_ge(x1T_ready, 1)
                act.activation(xs_hi[:, 0, 0:K], xT[:, 0, 0:K], ACT.Copy).then_inc(x1_hi_ready, 1)

            def group_hi(g):
                act.wait_ge(x1T_ready, g + 1)
                act.wait_ge(xaT_ready, g + 1)
                if g >= 2:
                    act.wait_ge(up_done, NC * (g - 1))
                k = slice(K, K + 2) if g == 0 else slice(0, K + 2)
                act.activation(xs_hi[:, g % 2, k], xT[:, g, k], ACT.Copy).then_inc(xs_hi_ready, 1)

            def b_hi(g, c):
                act.wait_ge(b_raw_in[g % 2][c], 16 * SG * (g // 2 + 1))
                if g == 0:
                    act.wait_ge(consts_ready, 2)
                if g >= 2:
                    act.wait_ge(up_done, NC * (g - 2) + c + 1)
                act.activation(b_part(b_grp[:, g % 2], c), b_part(b_raw[:, g % 2], c), ACT.Copy, scale=sign_lo[:]
                               ).then_inc(b_hi_ready, 1)

            def ad_hi(g):
                act.wait_ge(ad_grp_ready, g + 1)
                if g >= 2:
                    act.wait_ge(down_done, NC * (g - 1))
                act.activation(wdx[:, 0, :, ad_cols(g)], ad_grp[:, g % 2].rearrange("p t s r -> p t (s r)"),
                               ACT.Copy).then_inc(ad_hi_ready, 1)

            def bd_hi(g):
                act.wait_ge(bd_raw_in[g % 2], 16 * SG * (g // 2 + 1))
                if g >= 2:
                    act.wait_ge(y_done, g - 1)
                act.activation(bd_grp[:, g % 2], bd_raw[:, g % 2], ACT.Copy, scale=sign_lo[:]).then_inc(bd_hi_ready, 1)

            def silu(q):
                act.wait_ge(gate_done, q + 1)
                if q >= 2:
                    act.wait_ge(h_ready, q - 1)
                act.activation(sg[:, q % 2], gate_ps[q % 2][:], ACT.Silu).then_inc(silu_ready, 1)

            def hidden_hi(q):
                act.wait_ge(hT_done, q + 1)
                if q >= 2:
                    act.wait_ge(down_done, q - 1)
                for ts in hidden_parts(q):
                    act.activation(hT_hi[:, q % 2, ts], hT_at(q, ts), ACT.Copy).then_inc(hT_hi_ready, 1)

            def rank_hi(g):
                act.wait_ge(xdT_done, g + 1)
                if g + 3 < G:
                    act.wait_ge(xaT_done, g + 4)
                if g >= 1:
                    act.wait_ge(y_done, g)
                act.activation(xd_hi[:], side_ps[:, 0:P], ACT.Copy).then_inc(xd_hi_ready, 1)

            weight_hi(0)
            x1T_out(0)
            x1_hi_first()
            x1T_out(1)
            weight_hi(1)
            b_hi(0, 0)
            xaT_out(0)
            group_hi(0)
            weight_hi(2)
            weight_hi(3)
            silu(0)
            b_hi(0, 1)
            xaT_out(1)
            x1T_out(2)
            group_hi(1)
            hidden_hi(0)
            weight_hi(4)
            ad_hi(0)
            silu(1)
            b_hi(1, 0)
            xaT_out(2)
            weight_hi(5)

            for q in range(2, Q + 1):
                g, c = q // NC, q % NC
                if q == 2:
                    hidden_hi(q - 1)
                if q < Q:
                    silu(q)
                if q > 2:
                    hidden_hi(q - 1)
                if c == 1:
                    rank_hi(g - 1)
                if c == 1 and g + 2 < G:
                    xaT_out(g + 2)
                if q == 2:
                    x1T_out(3)
                    b_hi(1, 1)
                    ad_hi(1)
                    bd_hi(0)
                    group_hi(2)
                    b_hi(2, 0)
                if q == 3:
                    bd_hi(1)
                if q == 4:
                    b_hi(2, 1)
                if q >= 4 and c == 0 and g + 1 < G:
                    group_hi(g + 1)
                if q >= 4 and g + 1 < G:
                    b_hi(g + 1, c)
                if c == 1 and g + 1 < G:
                    ad_hi(g + 1)
                    bd_hi(g + 1)
                if q >= 4 and c == 0 and g + 2 < G:
                    x1T_out(g + 2)
            rank_hi(G - 1)

        @block.tensor
        def _(pe):
            def l0(g):
                pe.wait_ge(diag_ready, g + 1)
                if g % 2 == 0:
                    pe.wait_ge(x_in[g // 2], 16)
                if g >= 3:
                    pe.wait_ge(xaT_ready, g)
                if g >= 4:
                    pe.wait_ge(xd_lo_ready, g - 3)
                pe.matmul(l0_at(g), w0_diag[:, g].rearrange("p s c -> p (s c)"), x_sb[:, g],
                          start=True, stop=True).then_inc(l0_done, 1)

            def x1_turn(g):
                if g == 0:
                    pe.wait_ge(ident_ready, 1)
                pe.wait_ge(x1_ready, g + 1)
                for k in range(K):
                    mm = pe.transpose(x1T_at(g)[:, k * P:(k + 1) * P], x1[:, g, k], ident[:])
                mm.then_inc(x1T_done, 1)

            def rank_in(g):
                pe.wait_ge(x1T_ready, g + 1)
                pe.wait_ge(a_grp_ready, g + 1)
                for k in range(K):
                    mm = pe.matmul(a_at(g), xT[:, g, k],
                                   a_grp[:, g % 2, k].rearrange("p m s r -> p (m s r)"),
                                   start=(k == 0), stop=(k == K - 1))
                mm.then_inc(a_done, 1)

            def xa_turn(g):
                pe.wait_ge(xa_ready, g + 1)
                for m in range(2):
                    mm = pe.transpose(xaT_at(g)[:, m * P:(m + 1) * P],
                                      xa[:, g % 2, m].rearrange("p s l r -> p (s l r)"), ident[:])
                mm.then_inc(xaT_done, 1)

            def mlp_hi(q, mat, ps):
                g, c = q // NC, q % NC
                cols = slice(c * CH, (c + 1) * CH)
                if g == 0:
                    pe.wait_ge(split_hi, W_SPLIT[mat, c])
                for k in range(K):
                    pe.matmul(ps, xs_hi[:, g % 2, k], w_hi[:, mat, k, cols], start=(k == 0), stop=False)
                if q == 0 and mat == 0:
                    pe.wait_ge(x1_lo_ready, 1)
                for k in range(K):
                    pe.matmul(ps, xs_lo[:, g % 2, k], w_hi[:, mat, k, cols], start=False, stop=False)

            def mlp_lo(q, mat, ps):
                g, c = q // NC, q % NC
                cols = slice(c * CH, (c + 1) * CH)
                if g == 0:
                    pe.wait_ge(split_lo, W_SPLIT[mat, c])
                for k in range(K):
                    pe.matmul(ps, xs_hi[:, g % 2, k], w_lo[:, mat, k, cols], start=False, stop=False)

            def lora_part(q, mat, ps, done):
                g, c = q // NC, q % NC
                b = g % 2
                if mat == 0:
                    pe.wait_ge(b_ready, q + 1)
                rows = b_part(b_grp[:, b], c)[:, mat]
                pe.matmul(ps, xs_hi[:, b, K + mat], rows, start=False, stop=False)
                pe.matmul(ps, xs_lo[:, b, K + mat], rows, start=False, stop=True).then_inc(done, 1)

            def mlp_gate(q):
                g, c = q // NC, q % NC
                if g >= 1 and c == 0:
                    pe.wait_ge(xs_hi_ready, g + 1)
                    pe.wait_ge(xs_lo_ready, g + 1)
                if q >= 2:
                    pe.wait_ge(silu_ready, q - 1)
                mlp_hi(q, 0, gate_ps[q % 2][:])
                mlp_lo(q, 0, gate_ps[q % 2][:])

            def mlp_up(q):
                if q >= 2:
                    pe.wait_ge(h_ready, q - 1)
                mlp_hi(q, 1, up_ps[q % 2][:])
                mlp_lo(q, 1, up_ps[q % 2][:])

            def lora_gate(q):
                lora_part(q, 0, gate_ps[q % 2][:], gate_done)

            def lora_up(q):
                lora_part(q, 1, up_ps[q % 2][:], up_done)

            def hidden_turn(q):
                pe.wait_ge(h_ready, q + 1)
                if q == 0:
                    pe.wait_ge(xaT_ready, 1)
                else:
                    pe.wait_ge(hT_hi_ready, q)
                    pe.wait_ge(hT_lo_ready, q)
                for ts in hidden_parts(q):
                    for i in range(ts.stop - ts.start):
                        mm = pe.transpose(hT_at(q, ts)[:, i], h[:, q % 2, ts.start + i], ident[:])
                mm.then_inc(hT_done, 1)

            def down(q, tiles=range(T)):
                g, c = q // NC, q % NC
                if c == 0 and 0 in tiles:
                    pe.wait_ge(ad_lo_ready, g + 1)
                    if g >= 2:
                        pe.wait_ge(out_ready, g - 1)
                if g == 0:
                    pe.wait_ge(split_hi, WD_SPLIT[c])
                    pe.wait_ge(split_lo, WD_SPLIT[c])
                pe.wait_ge(hT_hi_ready, q + 1)
                pe.wait_ge(hT_lo_ready, q + 1)
                at = 0 if g % 2 == 0 else LR
                ps = y_ps[g % 2][:, 0:LR + D]
                for t in tiles:
                    kk = c * T + t
                    hi, lo = (wdx[:, l, kk, at:at + LR + D] for l in range(2))
                    pe.matmul(ps, hT_hi[:, q % 2, t], hi, start=(kk == 0), stop=False)
                    pe.matmul(ps, hT_hi[:, q % 2, t], lo, start=False, stop=False)
                    last = kk == KK - 1 or (q == Q - 2 and t == T - 1)
                    mm = pe.matmul(ps, hT_lo[:, q % 2, t], hi, start=False, stop=last)
                if T - 1 in tiles:
                    mm.then_inc(down_done, 1)

            def down_part(q, ps, cols, tiles, start, stop):
                for t in tiles:
                    if t % (T // 2) == 0:
                        pe.wait_ge(hT_hi_ready, q + 1 + t // (T // 2))
                        pe.wait_ge(hT_lo_ready, q + 1 + t // (T // 2))
                    kk = q % NC * T + t
                    hi, lo = (wdx[:, l, kk, cols] for l in range(2))
                    pe.matmul(ps, hT_hi[:, q % 2, t], hi, start=(start and t == 0), stop=False, skip_group_check=True)
                    pe.matmul(ps, hT_hi[:, q % 2, t], lo, start=False, stop=False, skip_group_check=True)
                    mm = pe.matmul(ps, hT_lo[:, q % 2, t], hi, start=False, stop=(stop and t == T - 1),
                                   skip_group_check=True)
                return mm

            def rank_turn(g):
                pe.wait_ge(xd_ready, g + 1)
                if g >= 1:
                    pe.wait_ge(xd_lo_ready, g)
                if g + 3 < G:
                    pe.wait_ge(xa_ready, g + 4)
                pe.transpose(side_ps[:, 0:P], xd[:].rearrange("p s l r -> p (s l r)"), ident[:]).then_inc(xdT_done, 1)

            def rank_out(g):
                pe.wait_ge(bd_grp_ready, g + 1)
                pe.wait_ge(xd_hi_ready, g + 1)
                pe.wait_ge(xd_lo_ready, g + 1)
                ps = last_y if g == G - 1 else y_ps[g % 2][:, out_cols(g)]
                pe.matmul(ps, xd_hi[:], bd_grp[:, g % 2], start=False, stop=False, skip_group_check=True)
                pe.matmul(ps, xd_lo[:], bd_grp[:, g % 2], start=False, stop=True,
                          skip_group_check=True).then_inc(y_done, 1)

            pe.wait_ge(warm_ready, 1)
            for _ in range(WARM):
                pe.matmul(side_ps[:, 0:P], pe_warm[:], pe_warm[:], start=True, stop=True)

            l0(0)
            l0(1)
            x1_turn(0)
            x1_turn(1)
            rank_in(0)
            pe.wait_ge(x1_hi_ready, 1)
            mlp_hi(0, 0, gate_ps[0][:])
            rank_in(1)
            xa_turn(0)
            mlp_lo(0, 0, gate_ps[0][:])
            mlp_up(0)
            pe.wait_ge(xs_hi_ready, 1)
            pe.wait_ge(xs_lo_ready, 1)
            lora_gate(0)
            lora_up(0)
            xa_turn(1)
            l0(2)
            mlp_gate(1)
            x1_turn(2)
            mlp_up(1)
            hidden_turn(0)
            rank_in(2)
            lora_gate(1)
            lora_up(1)
            mlp_gate(2)
            xa_turn(2)
            mlp_up(2)
            l0(3)
            down(0, range(T // 2))
            hidden_turn(1)
            down(0, range(T // 2, T))
            lora_gate(2)
            lora_up(2)
            x1_turn(3)
            down(1)
            rank_in(3)

            for q in range(3, Q):
                g, c = q // NC, q % NC
                n = g + 2
                mlp_gate(q)
                lora_gate(q)
                hidden_turn(q - 1)
                if c == 0 and n < G:
                    l0(n)
                if c == 1:
                    rank_turn(g - 1)
                if c == 1 and n < G:
                    xa_turn(n)
                mlp_up(q)
                lora_up(q)
                if c == 0 and n < G:
                    x1_turn(n)
                if c == 1:
                    rank_out(g - 1)
                if q < Q - 1:
                    down(q - 1)
                if c == 0 and n < G:
                    rank_in(n)

            down(Q - 2, range(T // 2))
            hidden_turn(Q - 1)
            down(Q - 2, range(T // 2, T))
            down_part(Q - 1, y_ps[(G - 1) % 2][:, rank_cols(G - 1)], ad_cols(G - 1), range(T), False, True
                      ).then_inc(last_rank_done, 1)
            down_part(Q - 1, last_y, WD, range(T // 2), True, False)
            rank_turn(G - 1)
            down_part(Q - 1, last_y, WD, range(T // 2, T), False, False)
            rank_out(G - 1)

        @block.vector
        def _(dve):
            dve.memset(pe_warm[:], 0.0).then_inc(warm_ready, 1)
            dve.memset(own[:], 0.0).then_inc(dve_step, 1)
            dve.wait_ge(dve_step, 1)
            for s in range(SG):
                last = dve.memset(own[s * C:(s + 1) * C, s:2 * SG:SG], 1.0)
            last.then_inc(own_ready, 1)
            dve.wait_ge(row_ready, 1)
            dve.tensor_scalar(row_bit[:], row[:], R, None, ALU.bitwise_and).then_inc(dve_step, 1)
            dve.wait_ge(dve_step, 2)
            dve.tensor_scalar(is_lo[:], row_bit[:], 1.0 / R, None, ALU.mult).then_inc(consts_ready, 1)
            dve.tensor_scalar(sign_lo[:], row_bit[:], -2.0 / R, 1.0, ALU.mult, ALU.add).then_inc(consts_ready, 1)

            def diagonal(g):
                if g == 0:
                    dve.wait_ge(own_ready, 1)
                dve.wait_ge(w0_own_ready, g + 1)
                dve.tensor_tensor(w0_diag[:, g], w0_own[:, g], own[:, 0:SG].unsqueeze(2).to_broadcast([P, SG, C]),
                                  ALU.mult).then_inc(diag_ready, 1)

            def x1_add(g):
                dve.wait_ge(l0_done, g + 1)
                dve.tensor_tensor(x1[:, g], by_tile(l0_at(g)), by_tile(x_sb[:, g]),
                                  ALU.add).then_inc(x1_ready, 1)

            def xa_place(g):
                dve.wait_ge(a_done, g + 1)
                if g >= 2:
                    dve.wait_ge(xaT_done, g - 1)
                dve.tensor_tensor(
                    xa[:, g % 2].rearrange("p m s l r -> p (m s) l r"),
                    a_at(g).rearrange("p (j r) -> p j r", r=R).unsqueeze(2)
                    .to_broadcast([P, 2 * SG, 2, R]),
                    own[:].unsqueeze(2).unsqueeze(3).to_broadcast([P, 2 * SG, 2, R]), ALU.mult).then_inc(xa_ready, 1)

            def weight_lo(i):
                raw, hi, lo, _ = splits[i]
                dve.wait_ge(split_hi, i + 1)
                dve.tensor_tensor(lo, raw, hi.bitcast(F32), ALU.subtract).then_inc(split_lo, 1)

            def b_lo(g, c):
                dve.wait_ge(b_hi_ready, NC * g + c + 1)
                rows = b_part(b_grp[:, g % 2], c)
                dve.scalar_tensor_tensor(out=rows, in0=b_part(b_raw[:, g % 2], c), scalar=is_lo[:],
                                         in1=rows.bitcast(F32), op0=ALU.mult, op1=ALU.add).then_inc(b_ready, 1)

            def ad_lo(g):
                dve.wait_ge(ad_hi_ready, g + 1)
                dve.tensor_tensor(wdx[:, 1, :, ad_cols(g)], ad_grp[:, g % 2].rearrange("p t s r -> p t (s r)"),
                                  wdx[:, 0, :, ad_cols(g)].bitcast(F32), ALU.subtract).then_inc(ad_lo_ready, 1)

            def bd_lo(g):
                dve.wait_ge(bd_hi_ready, g + 1)
                dve.scalar_tensor_tensor(out=bd_grp[:, g % 2], in0=bd_raw[:, g % 2], scalar=is_lo[:],
                                         in1=bd_grp[:, g % 2].bitcast(F32), op0=ALU.mult, op1=ALU.add
                                         ).then_inc(bd_grp_ready, 1)

            def x1_lo_first():
                dve.wait_ge(x1_hi_ready, 1)
                dve.tensor_tensor(xs_lo[:, 0, 0:K], xT[:, 0, 0:K], xs_hi[:, 0, 0:K].bitcast(F32),
                                  ALU.subtract).then_inc(x1_lo_ready, 1)

            def group_lo(g):
                dve.wait_ge(xs_hi_ready, g + 1)
                k = slice(K, K + 2) if g == 0 else slice(0, K + 2)
                dve.tensor_tensor(xs_lo[:, g % 2, k], xT[:, g, k], xs_hi[:, g % 2, k].bitcast(F32),
                                  ALU.subtract).then_inc(xs_lo_ready, 1)

            def hidden_lo(q):
                for i, ts in enumerate(hidden_parts(q)):
                    dve.wait_ge(hT_hi_ready, q + 1 + i)
                    dve.tensor_tensor(hT_lo[:, q % 2, ts], hT_at(q, ts),
                                      hT_hi[:, q % 2, ts].bitcast(F32), ALU.subtract).then_inc(hT_lo_ready, 1)

            def hidden(q):
                dve.wait_ge(silu_ready, q + 1)
                dve.wait_ge(up_done, q + 1)
                if q >= 2:
                    dve.wait_ge(hT_done, q - 1)
                dve.tensor_tensor(h[:, q % 2], up_ps[q % 2][:].rearrange("n (p t) -> n t p", t=T),
                                  sg[:, q % 2].rearrange("n (p t) -> n t p", t=T), ALU.mult).then_inc(h_ready, 1)

            def rank_place(g):
                if g < G - 1:
                    dve.wait_ge(down_done, NC * (g + 1))
                else:
                    dve.wait_ge(last_rank_done, 1)
                if g >= 1:
                    dve.wait_ge(xdT_done, g)
                dve.tensor_tensor(
                    xd[:], y_ps[g % 2][:, rank_cols(g)].rearrange("p (s r) -> p s r", s=SG).unsqueeze(2)
                    .to_broadcast([P, SG, 2, R]),
                    own[:, 0:SG].unsqueeze(2).unsqueeze(3).to_broadcast([P, SG, 2, R]), ALU.mult).then_inc(xd_ready, 1)

            def rank_lo(g):
                dve.wait_ge(xd_hi_ready, g + 1)
                if g + 3 < G:
                    dve.wait_ge(xaT_ready, g + 4)
                dve.tensor_tensor(xd_lo[:], side_ps[:, 0:P], xd_hi[:].bitcast(F32),
                                  ALU.subtract).then_inc(xd_lo_ready, 1)

            def final(g):
                dve.wait_ge(y_done, g + 1)
                if g >= 2:
                    dve.wait_ge(out_sent[g % 2], 16 * (g // 2))
                if g == G - 1:
                    dve.wait_ge(last_sum_ready, 1)
                y = last_y if g == G - 1 else y_ps[g % 2][:, out_cols(g)]
                dve.tensor_tensor(by_tile(out_sb[:, g % 2]), by_tile(y), x1[:, g], ALU.add).then_inc(out_ready, 1)

            diagonal(0)
            diagonal(1)
            x1_add(0)
            x1_add(1)
            weight_lo(0)
            x1_lo_first()
            xa_place(0)
            weight_lo(1)
            b_lo(0, 0)
            group_lo(0)
            xa_place(1)
            diagonal(2)
            weight_lo(2)
            x1_add(2)
            weight_lo(3)
            hidden(0)
            b_lo(0, 1)
            group_lo(1)
            hidden_lo(0)
            xa_place(2)
            weight_lo(4)
            ad_lo(0)
            diagonal(3)
            hidden(1)
            b_lo(1, 0)
            weight_lo(5)

            for q in range(2, Q + 1):
                g, c = q // NC, q % NC
                n = g + 2
                if c == 1 and q > 3:
                    rank_place(g - 1)
                if c == 0 and n < G:
                    x1_add(n)
                hidden_lo(q - 1)
                if c == 1:
                    rank_lo(g - 1)
                if q < Q:
                    hidden(q)
                if c == 1:
                    final(g - 1)
                if q == 2:
                    b_lo(1, 1)
                    ad_lo(1)
                    bd_lo(0)
                    xa_place(3)
                    rank_place(0)
                    group_lo(2)
                if q == 3:
                    b_lo(2, 0)
                if q == 4:
                    b_lo(2, 1)
                if q >= 4 and c == 0 and g + 1 < G:
                    group_lo(g + 1)
                if q >= 4 and g + 1 < G:
                    b_lo(g + 1, c)
                if c == 1 and g + 3 < G:
                    diagonal(g + 3)
                if c == 1 and g + 1 < G:
                    ad_lo(g + 1)
                    if q == 3:
                        bd_lo(1)
                    bd_lo(g + 1)
                if q > 2 and c == 0 and n < G:
                    xa_place(n)
            rank_place(G - 1)
            dve.tensor_tensor(x1[:, G - 1], by_tile(y_ps[(G - 1) % 2][:, out_cols(G - 1)]), x1[:, G - 1],
                              ALU.add).then_inc(last_sum_ready, 1)
            rank_lo(G - 1)
            final(G - 1)


def kernel(x, itok_B_0_7, L0_cond_weights, L1_cond_Wg, L1_cond_Wu, L1_cond_Wd, L1_cond_Ag, L1_cond_Bg,
           L1_cond_Au, L1_cond_Bu, L1_cond_Ad, L1_cond_Bd):
    import numpy as _np
    import concourse.bacc as _bacc
    from concourse import mybir as _mybir
    from concourse.bass_utils import run_bass_kernel_spmd as _run

    P, T = 128, 4
    N, D, R = L1_cond_Ag.shape
    I = L1_cond_Ad.shape[1]
    a_in = _np.stack([L1_cond_Ag, L1_cond_Au]).reshape(2, N, P, D // P, R).transpose(2, 0, 1, 3, 4)
    a_down = _np.reshape(L1_cond_Ad, (N, I // (P * T), P, T, R)).transpose(2, 0, 1, 3, 4).reshape(P, N, I // P, R)
    w0 = _np.transpose(L0_cond_weights, (1, 0, 2))
    C = w0.shape[0]
    b_all = _np.concatenate([L1_cond_Bg, L1_cond_Bu, L1_cond_Bd], axis=2)
    data = {
        "x": x, "idx": itok_B_0_7, "w0": _np.concatenate([w0] * (P // C)),
        "Wg": L1_cond_Wg, "Wu": L1_cond_Wu, "Wd": L1_cond_Wd, "A_in": a_in,
        "B_all": _np.concatenate([b_all, b_all], axis=1), "A_down": a_down,
    }
    nc = _bacc.Bacc("TRN2", target_bir_lowering=False, num_devices=1)
    arrays, args = {}, []
    for name, a in data.items():
        a = _np.ascontiguousarray(a)
        arrays[f"in_{name}"] = a
        args.append(nc.dram_tensor(f"in_{name}", a.shape, _mybir.dt.from_np(a.dtype), kind="ExternalInput").ap())
    args.append(nc.dram_tensor("out_dram", x.shape, _mybir.dt.float32, kind="ExternalOutput").ap())
    cond_resid_kernel(nc, *args)
    r = _run(nc, [arrays], core_ids=[0])
    return r.results[0]["out_dram"]
```
